# Optimizing a Trainium2 kernel written in Bass

```python
import numpy as np
import jax
import jax.numpy as jnp

def _softmax(x, axis=-1):
    return jax.nn.softmax(x, axis=axis)

def _gelu(x):
    return jax.nn.gelu(x, approximate=True)

def _silu(x):
    return jax.nn.silu(x)

def _sigmoid(x):
    return jax.nn.sigmoid(x)

def _layernorm(x, axis=-1, eps=1e-05):
    m = jnp.mean(x, axis=axis, keepdims=True)
    v = jnp.var(x, axis=axis, keepdims=True)
    return (x - m) / jnp.sqrt(v + eps)

def _scatter_add(tgt, idx, src, axis=0):
    return tgt.at[idx].add(src)

def _segment_sum(src, seg, n):
    return jax.ops.segment_sum(src, seg, n)
kernel_name = 'mk_conv_attn_hybrid_d2_conv_nhwc256_r4_432037'

def setup_inputs(seed: int=0):
    np.random.seed(seed)
    _w = jnp.asarray

    def _rec_inputs():
        import jax
        import jax.numpy as jnp
        _gk = jax.random.key(seed)
        x = -0.0002928 + 1 * jax.random.normal(jax.random.fold_in(_gk, 1), (4, 16, 16, 64), jnp.float32)
        return x
    x = _rec_inputs()

    def _L0_conv_setup():
        import jax, jax.numpy as jnp
        import numpy as np
        from jax import lax
        K_SIZE = 3
        STRIDE = 1
        PADDING = 1

        def _dcnv2(x, offset_w, offset_b, dcn_weight):
            k, stride, padding = (K_SIZE, STRIDE, PADDING)
            N, H, W, C = x.shape
            kk = k * k
            om = lax.conv_general_dilated(x, offset_w, window_strides=(stride, stride), padding='SAME', dimension_numbers=('NHWC', 'HWIO', 'NHWC')) + offset_b
            offset = om[..., :2 * kk]
            mask = jax.nn.sigmoid(om[..., 2 * kk:])
            oH = (H + 2 * padding - (k - 1)) // stride
            oW = (W + 2 * padding - (k - 1)) // stride
            pad_x = jnp.pad(x, ((0, 0), (padding, padding + 1), (padding, padding + 1), (0, 0)))
            base_y = jnp.arange(oH, dtype=x.dtype) * stride + padding
            base_x = jnp.arange(oW, dtype=x.dtype) * stride + padding
            kr = jnp.arange(k, dtype=x.dtype) - (k - 1) / 2.0
            inner_y = jnp.repeat(kr, k)
            inner_x = jnp.tile(kr, k)
            off_yx = offset.reshape(N, oH, oW, kk, 2)
            pos_y = base_y[None, :, None, None] + inner_y[None, None, None, :] + off_yx[..., 0]
            pos_x = base_x[None, None, :, None] + inner_x[None, None, None, :] + off_yx[..., 1]
            pos_y = jnp.clip(pos_y, 0.0, H + 2 * padding - 1.0)
            pos_x = jnp.clip(pos_x, 0.0, W + 2 * padding - 1.0)
            y1 = jnp.floor(pos_y)
            x1 = jnp.floor(pos_x)
            y1i = y1.astype(jnp.int32)
            x1i = x1.astype(jnp.int32)
            y2i = y1i + 1
            x2i = x1i + 1
            gather = jax.vmap(lambda px, yi, xi: px[yi, xi])
            v1 = gather(pad_x, y1i, x1i)
            v2 = gather(pad_x, y1i, x2i)
            v3 = gather(pad_x, y2i, x1i)
            v4 = gather(pad_x, y2i, x2i)
            lh = (pos_y - y1)[..., None]
            lw = (pos_x - x1)[..., None]
            hh = 1.0 - lh
            hw = 1.0 - lw
            value = (hh * hw * v1 + hh * lw * v2 + lh * hw * v3 + lh * lw * v4) * mask[..., None]
            value = jnp.transpose(value, (0, 1, 2, 4, 3)).reshape(N, oH, oW, C * kk)
            w = jnp.transpose(dcn_weight, (1, 2, 3, 0)).reshape(C * kk, -1)
            return jnp.einsum('nhwc,cf->nhwf', value, w)
        key = jax.random.key(seed)
        k1, k2, k3 = jax.random.split(key, 3)
        x = jax.random.normal(k1, (4, 16, 16, 64), dtype=jnp.float32)
        offset_w = jax.random.normal(k2, (3, 3, 64, 27), dtype=jnp.float32) * 0.01
        offset_b = jnp.zeros((1, 1, 1, 27), dtype=jnp.float32)
        dcn_weight = jax.random.normal(k3, (64, 64, 3, 3), dtype=jnp.float32) * 0.02
        return {'x': x, 'offset_w': offset_w, 'offset_b': offset_b, 'dcn_weight': dcn_weight}
    _L0_conv_all = _L0_conv_setup()
    _L0_conv_in = {k: v for k, v in _L0_conv_all.items() if k in ('offset_w', 'offset_b', 'dcn_weight')}
    del _L0_conv_all

    def _L1_attn_setup():
        import jax, jax.numpy as jnp
        import numpy as np
        H = 8
        HD = 32
        LN_EPS = 1e-05

        def _layernorm(x, g, b):
            m = jnp.mean(x, axis=-1, keepdims=True)
            v = jnp.mean(jnp.square(x - m), axis=-1, keepdims=True)
            return (x - m) * jax.lax.rsqrt(v + LN_EPS) * g + b
        key = jax.random.key(seed)
        ks = jax.random.split(key, 8)
        D, DFF = (64, 256)
        B, N = (8, 512)
        s = 0.02
        return {'x': jax.random.normal(ks[0], (B, N, D), jnp.float32), 'w_qkv': jax.random.normal(ks[1], (3 * H * HD, D), jnp.float32) * s, 'w_out': jax.random.normal(ks[2], (D, H * HD), jnp.float32) * s, 'b_out': jnp.zeros((D,), jnp.float32), 'w1': jax.random.normal(ks[3], (DFF, D), jnp.float32) * s, 'wv': jax.random.normal(ks[4], (DFF, D), jnp.float32) * s, 'w2': jax.random.normal(ks[5], (D, DFF), jnp.float32) * s, 'ln1_g': jnp.ones((D,), jnp.float32), 'ln1_b': jnp.zeros((D,), jnp.float32), 'ln2_g': jnp.ones((D,), jnp.float32), 'ln2_b': jnp.zeros((D,), jnp.float32)}
    _L1_attn_all = _L1_attn_setup()
    _L1_attn_in = {k: v for k, v in _L1_attn_all.items() if k in ('w_qkv', 'w_out', 'b_out', 'w1', 'wv', 'w2', 'ln1_g', 'ln1_b', 'ln2_g', 'ln2_b')}
    del _L1_attn_all

    def _L1_ffn_setup():
        import jax, jax.numpy as jnp
        import numpy as np
        from jax import lax
        key = jax.random.key(seed)
        B, T, I, H = (16, 512, 64, 64)
        ks = jax.random.split(key, 13)
        s = 1.0 / np.sqrt(H)

        def w(k, shape):
            return jax.random.uniform(k, shape, jnp.float32, -s, s)
        return {'x': jax.random.normal(ks[0], (B, T, I), jnp.float32), 'U_i': w(ks[1], (I, H)), 'V_i': w(ks[2], (H, H)), 'b_i': w(ks[3], (H,)), 'U_f': w(ks[4], (I, H)), 'V_f': w(ks[5], (H, H)), 'b_f': w(ks[6], (H,)), 'U_c': w(ks[7], (I, H)), 'V_c': w(ks[8], (H, H)), 'b_c': w(ks[9], (H,)), 'U_o': w(ks[10], (I, H)), 'V_o': w(ks[11], (H, H)), 'b_o': w(ks[12], (H,))}
    _L1_ffn_all = _L1_ffn_setup()
    _L1_ffn_in = {k: v for k, v in _L1_ffn_all.items() if k in ('U_i', 'V_i', 'b_i', 'U_f', 'V_f', 'b_f', 'U_c', 'V_c', 'b_c', 'U_o', 'V_o', 'b_o')}
    del _L1_ffn_all
    return {'x': x, 'L0_conv_offset_w': _L0_conv_in['offset_w'], 'L0_conv_offset_b': _L0_conv_in['offset_b'], 'L0_conv_dcn_weight': _L0_conv_in['dcn_weight'], 'L1_attn_w_qkv': _L1_attn_in['w_qkv'], 'L1_attn_w_out': _L1_attn_in['w_out'], 'L1_attn_b_out': _L1_attn_in['b_out'], 'L1_attn_w1': _L1_attn_in['w1'], 'L1_attn_wv': _L1_attn_in['wv'], 'L1_attn_w2': _L1_attn_in['w2'], 'L1_attn_ln1_g': _L1_attn_in['ln1_g'], 'L1_attn_ln1_b': _L1_attn_in['ln1_b'], 'L1_attn_ln2_g': _L1_attn_in['ln2_g'], 'L1_attn_ln2_b': _L1_attn_in['ln2_b'], 'L1_ffn_U_i': _L1_ffn_in['U_i'], 'L1_ffn_V_i': _L1_ffn_in['V_i'], 'L1_ffn_b_i': _L1_ffn_in['b_i'], 'L1_ffn_U_f': _L1_ffn_in['U_f'], 'L1_ffn_V_f': _L1_ffn_in['V_f'], 'L1_ffn_b_f': _L1_ffn_in['b_f'], 'L1_ffn_U_c': _L1_ffn_in['U_c'], 'L1_ffn_V_c': _L1_ffn_in['V_c'], 'L1_ffn_b_c': _L1_ffn_in['b_c'], 'L1_ffn_U_o': _L1_ffn_in['U_o'], 'L1_ffn_V_o': _L1_ffn_in['V_o'], 'L1_ffn_b_o': _L1_ffn_in['b_o']}

def reference(x, L0_conv_offset_w, L0_conv_offset_b, L0_conv_dcn_weight, L1_attn_w_qkv, L1_attn_w_out, L1_attn_b_out, L1_attn_w1, L1_attn_wv, L1_attn_w2, L1_attn_ln1_g, L1_attn_ln1_b, L1_attn_ln2_g, L1_attn_ln2_b, L1_ffn_U_i, L1_ffn_V_i, L1_ffn_b_i, L1_ffn_U_f, L1_ffn_V_f, L1_ffn_b_f, L1_ffn_U_c, L1_ffn_V_c, L1_ffn_b_c, L1_ffn_U_o, L1_ffn_V_o, L1_ffn_b_o):
    import jax
    import jax.numpy as jnp

    def _L0_conv_ref(x, offset_w, offset_b, dcn_weight):
        import jax, jax.numpy as jnp
        import numpy as np
        from jax import lax
        K_SIZE = 3
        STRIDE = 1
        PADDING = 1

        def _dcnv2(x, offset_w, offset_b, dcn_weight):
            k, stride, padding = (K_SIZE, STRIDE, PADDING)
            N, H, W, C = x.shape
            kk = k * k
            om = lax.conv_general_dilated(x, offset_w, window_strides=(stride, stride), padding='SAME', dimension_numbers=('NHWC', 'HWIO', 'NHWC')) + offset_b
            offset = om[..., :2 * kk]
            mask = jax.nn.sigmoid(om[..., 2 * kk:])
            oH = (H + 2 * padding - (k - 1)) // stride
            oW = (W + 2 * padding - (k - 1)) // stride
            pad_x = jnp.pad(x, ((0, 0), (padding, padding + 1), (padding, padding + 1), (0, 0)))
            base_y = jnp.arange(oH, dtype=x.dtype) * stride + padding
            base_x = jnp.arange(oW, dtype=x.dtype) * stride + padding
            kr = jnp.arange(k, dtype=x.dtype) - (k - 1) / 2.0
            inner_y = jnp.repeat(kr, k)
            inner_x = jnp.tile(kr, k)
            off_yx = offset.reshape(N, oH, oW, kk, 2)
            pos_y = base_y[None, :, None, None] + inner_y[None, None, None, :] + off_yx[..., 0]
            pos_x = base_x[None, None, :, None] + inner_x[None, None, None, :] + off_yx[..., 1]
            pos_y = jnp.clip(pos_y, 0.0, H + 2 * padding - 1.0)
            pos_x = jnp.clip(pos_x, 0.0, W + 2 * padding - 1.0)
            y1 = jnp.floor(pos_y)
            x1 = jnp.floor(pos_x)
            y1i = y1.astype(jnp.int32)
            x1i = x1.astype(jnp.int32)
            y2i = y1i + 1
            x2i = x1i + 1
            gather = jax.vmap(lambda px, yi, xi: px[yi, xi])
            v1 = gather(pad_x, y1i, x1i)
            v2 = gather(pad_x, y1i, x2i)
            v3 = gather(pad_x, y2i, x1i)
            v4 = gather(pad_x, y2i, x2i)
            lh = (pos_y - y1)[..., None]
            lw = (pos_x - x1)[..., None]
            hh = 1.0 - lh
            hw = 1.0 - lw
            value = (hh * hw * v1 + hh * lw * v2 + lh * hw * v3 + lh * lw * v4) * mask[..., None]
            value = jnp.transpose(value, (0, 1, 2, 4, 3)).reshape(N, oH, oW, C * kk)
            w = jnp.transpose(dcn_weight, (1, 2, 3, 0)).reshape(C * kk, -1)
            return jnp.einsum('nhwc,cf->nhwf', value, w)
        return _dcnv2(x, offset_w, offset_b, dcn_weight)

    def _L1_attn_ref(x, w_qkv, w_out, b_out, w1, wv, w2, ln1_g, ln1_b, ln2_g, ln2_b):
        import jax, jax.numpy as jnp
        import numpy as np
        H = 8
        HD = 32
        LN_EPS = 1e-05

        def _layernorm(x, g, b):
            m = jnp.mean(x, axis=-1, keepdims=True)
            v = jnp.mean(jnp.square(x - m), axis=-1, keepdims=True)
            return (x - m) * jax.lax.rsqrt(v + LN_EPS) * g + b
        B, N, D = x.shape
        scale = HD ** (-0.5)
        qkv = x @ w_qkv.T
        q, k, v = jnp.split(qkv, 3, axis=-1)

        def to_heads(t):
            return t.reshape(B, N, H, HD).transpose(0, 2, 1, 3)
        q, k, v = (to_heads(q), to_heads(k), to_heads(v))
        sim = jnp.einsum('bhid,bhjd->bhij', q, k) * scale
        attn = jax.nn.softmax(sim, axis=-1)
        o = jnp.einsum('bhij,bhjd->bhid', attn, v)
        o = o.transpose(0, 2, 1, 3).reshape(B, N, H * HD)
        y = o @ w_out.T + b_out
        x1 = _layernorm(y + x, ln1_g, ln1_b)
        ff = jax.nn.gelu(y @ w1.T, approximate=False) * (y @ wv.T)
        ff = ff @ w2.T
        return _layernorm(ff + x1, ln2_g, ln2_b)

    def _L1_ffn_ref(x, U_i, V_i, b_i, U_f, V_f, b_f, U_c, V_c, b_c, U_o, V_o, b_o):
        import jax, jax.numpy as jnp
        import numpy as np
        from jax import lax
        B, T, _ = x.shape
        H = U_i.shape[1]
        xt = jnp.swapaxes(x, 0, 1)
        xi = xt @ U_i + b_i
        xf = xt @ U_f + b_f
        xg = xt @ U_c + b_c
        xo = xt @ U_o + b_o
        h0 = jnp.zeros((B, H), x.dtype)
        c0 = jnp.zeros((B, H), x.dtype)

        def step(carry, xs):
            h, c = carry
            xi_t, xf_t, xg_t, xo_t = xs
            i_t = jax.nn.sigmoid(xi_t + h @ V_i)
            f_t = jax.nn.sigmoid(xf_t + h @ V_f)
            g_t = jnp.tanh(xg_t + h @ V_c)
            o_t = jax.nn.sigmoid(xo_t + h @ V_o)
            c_new = h * c + i_t * g_t
            h_new = o_t * jnp.tanh(c_new)
            return ((h_new, c_new), h_new)
        (_, _), hs = lax.scan(step, (h0, c0), (xi, xf, xg, xo))
        return jnp.swapaxes(hs, 0, 1)

    def _gn(v, G=32, eps=1e-05):
        B_, H_, W_, C_ = v.shape
        g = v.reshape(B_, H_, W_, G, C_ // G)
        m = jnp.mean(g, axis=(1, 2, 4), keepdims=True)
        s = jnp.var(g, axis=(1, 2, 4), keepdims=True)
        return ((g - m) / jnp.sqrt(s + eps)).reshape(v.shape)

    def _ln_c(v, eps=1e-06):
        m = jnp.mean(v, axis=-1, keepdims=True)
        s = jnp.var(v, axis=-1, keepdims=True)
        return (v - m) / jnp.sqrt(s + eps)

    def _ln_t(v, eps=1e-05):
        m = jnp.mean(v, axis=-1, keepdims=True)
        s = jnp.var(v, axis=-1, keepdims=True)
        return (v - m) / jnp.sqrt(s + eps)

    def _to_tokens(v):
        B_, H_, W_, C_ = v.shape
        return v.reshape(B_, H_ * W_, C_)

    def _from_tokens(t, like):
        return t.reshape(like.shape)
    x = x + _L0_conv_ref(_gn(x), L0_conv_offset_w, L0_conv_offset_b, L0_conv_dcn_weight)
    t = _to_tokens(x)
    t = t + _L1_attn_ref(_ln_t(t), L1_attn_w_qkv, L1_attn_w_out, L1_attn_b_out, L1_attn_w1, L1_attn_wv, L1_attn_w2, L1_attn_ln1_g, L1_attn_ln1_b, L1_attn_ln2_g, L1_attn_ln2_b)
    t = t + _L1_ffn_ref(_ln_t(t), L1_ffn_U_i, L1_ffn_V_i, L1_ffn_b_i, L1_ffn_U_f, L1_ffn_V_f, L1_ffn_b_f, L1_ffn_U_c, L1_ffn_V_c, L1_ffn_b_c, L1_ffn_U_o, L1_ffn_V_o, L1_ffn_b_o)
    x = _from_tokens(t, x)
    return x

_drawn_inputs = setup_inputs


def setup_inputs(seed=0):
    import zlib

    import numpy as np

    out = dict(_drawn_inputs(seed))
    spreads = {'L0_conv_offset_b': (0.0, 0.1),
     'L1_attn_b_out': (0.0, 0.1),
     'L1_attn_ln1_g': (1.0, 0.2),
     'L1_attn_ln1_b': (0.0, 0.1),
     'L1_attn_ln2_g': (1.0, 0.2),
     'L1_attn_ln2_b': (0.0, 0.1)}
    factors = {'L1_attn_w_qkv': 8.0,
     'L1_attn_w_out': 8.0,
     'L1_attn_w1': 8.0,
     'L1_attn_wv': 8.0,
     'L1_attn_w2': 8.0,
     'L1_ffn_U_i': 3.742,
     'L1_ffn_V_i': 8.0,
     'L1_ffn_b_i': 8.0,
     'L1_ffn_V_c': 7.553,
     'L1_ffn_b_c': 6.356,
     'L1_ffn_U_o': 3.56,
     'L1_ffn_V_o': 8.0,
     'L1_ffn_b_o': 8.0}
    for name, (base, spread) in spreads.items():
        noise = np.random.default_rng([zlib.crc32(name.encode()), seed]).standard_normal(out[name].shape)
        drawn = base * np.exp(spread * noise) if base else spread * noise
        out[name] = jnp.asarray(drawn.astype(out[name].dtype))
    for name, factor in factors.items():
        out[name] = (out[name] * factor).astype(out[name].dtype)
    return out
```

```python
from contextlib import ExitStack

import numpy as np

import concourse.bass as bass
from concourse import mybir

F32 = mybir.dt.float32
BF16 = mybir.dt.bfloat16
ALU = mybir.AluOpType
ACT = mybir.ActivationFunctionType
AX = mybir.AxisListType

P = 128
B, SIDE, C = 4, 16, 64
N = SIDE * SIDE
TAPS = 9
OFFS = 3 * TAPS
HALVES = N // P
HEADS, HD = 8, 32
HG = HEADS * HD // P
HPG = HEADS // HG
DFF = 256
FT = DFF // P
TT = 32
NT = N // TT
STEPS = TT
CHUNK = 16
LEAD = 38
OUT_LAG = 2
GN_EPS = LN_EPS = 1e-5
STEP_COLS = 1800

K_ID, K_PAIR, K_MASK, K_BASE, K_GRID = 0, 128, 256, 260, 296
K_END = 312
CW_OW, CW_DW = 0, TAPS * 2 * OFFS
CW_OB = CW_DW + TAPS * C
CW_END = CW_OB + 1
AW_QKV, AW_OUT, AW_W1, AW_WV = 0, 768, 768 + HG * C, 768 + HG * C + DFF
AW_W2 = AW_WV + DFF
AW_BO = AW_W2 + FT * C
AW_END = AW_BO + 1
LW_V, LW_U, LW_END = 0, 3 * C, 6 * C
VEC_BO, VEC_G1, VEC_B1, VEC_G2, VEC_B2 = range(5)


def hybrid_kernel(nc, x_fm2, x_fm, conv_w, attn_w, lstm_w, vecs, consts, out):
    ctx = ExitStack()
    with ctx:
        def sb(name, shape, dt=F32):
            return ctx.enter_context(nc.sbuf_tensor(name, shape, dt))

        def bank(name):
            return ctx.enter_context(nc.psum_tensor(name, [P, 512], F32))

        def sem(name):
            return ctx.enter_context(nc.semaphore(name))

        X2 = sb("X2", [P, 2, N])
        X = sb("X", [C, B, N])
        CW = sb("CW", [P, CW_END])
        AW = sb("AW", [P, AW_END])
        LW = sb("LW", [C + 1, LW_END])
        VEC = sb("VEC", [P, 5, C])
        K = sb("K", [P, K_END])
        ident = K[:, K_ID:K_ID + P]
        pair = K[:, K_PAIR:K_PAIR + P]
        head_mask = K[:, K_MASK:K_MASK + HPG]
        base = K[:, K_BASE:K_BASE + 36].rearrange("p (h k d) -> p h k d", h=2, d=2)
        grid = K[:, K_GRID:K_GRID + SIDE]
        OW = CW[:, CW_OW:CW_DW].rearrange("p (t o) -> p t o", t=TAPS)
        DW = CW[:, CW_DW:CW_OB]
        OB = CW[0:2 * OFFS, CW_OB:CW_OB + 1]

        gstat = sb("gstat", [P, 2, 6])
        gmv = sb("gmv", [P, 2, 2])
        gsq = sb("gsq", [P, 2, 1])
        gme = sb("gme", [P, 2, 2])
        gvar = sb("gvar", [P, 2, 1])
        grs = sb("grs", [P, 2, 1])
        XN = sb("XN", [P, 2, SIDE + 2, SIDE + 2])
        XC = sb("XC", [P, 2, N])
        OM = sb("OM", [2 * OFFS, 2, N])
        POS = sb("POS", [P, 2, B, TAPS, HALVES])
        MK = sb("MK", [P, B, TAPS, HALVES])
        HAT = sb("HAT", [P, 2, B, TAPS, HALVES, SIDE])
        A = sb("A", [P, 4, HALVES, N])
        AT = sb("AT", [P, 4, 2, HALVES, P])
        Z = sb("Z", [P, 2, B, TAPS, C])
        T0F = sb("T0F", [C, NT, B, TT])
        T0 = sb("T0", [P, NT, C])
        st0 = sb("st0", [P, NT, 6])
        mv0 = sb("mv0", [P, NT, 2])
        rs0 = sb("rs0", [P, NT, 1])
        Y = sb("Y", [P, NT, C])
        YB = sb("YB", [P, NT, C])
        TB = sb("TB", [P, NT, C])
        YF = sb("YF", [C, B, N])
        KF = sb("KF", [P, HG, B, N])
        V = sb("V", [P, B, HALVES, HEADS * HD])
        QB = sb("QB", [P, HG, B, HPG, TT])
        nmax = sb("nmax", [P, 2])
        rsum = sb("rsum", [P, 2])
        rinv = sb("rinv", [P, 2])
        E = sb("E", [P, 2, N])
        ET = sb("ET", [P, 2, HALVES, P])
        O = sb("O", [P, HG, B, TT])
        AY = sb("AY", [C, P])
        R1 = sb("R1", [P, C])
        R2 = sb("R2", [P, C])
        X1 = sb("X1", [P, C])
        GE = sb("GE", [P, FT, P])
        FF = sb("FF", [P, FT, P])
        st = sb("st", [P, 3, 6])
        mv = sb("mv", [P, 3, 2])
        rs = sb("rs", [P, 3, 1])
        half_neg = sb("half_neg", [P, NT])
        T1 = sb("T1", [P, NT, C])
        LN3 = sb("LN3", [P, C])
        XT = sb("XT", [C + 1, NT, B, TT])
        VW = sb("VW", [P, 3, C])
        UW = sb("UW", [C + 1, 3, C])
        H = sb("H", [P, STEPS, B])
        HF = sb("HF", [C, B, TT])
        SA = sb("SA", [C, 2, B, 4])
        CS = sb("CS", [C, B, 4])
        TO = sb("TO", [C, B])
        OUT = sb("OUT", [P, 2, C])
        FB = sb("FB", [P, 512], BF16)

        banks = [bank(f"bank{i}") for i in range(8)]
        b_misc, b_om, b_omt = banks[0], banks[1], banks[2]
        b_z = banks[3:7]
        b_at = banks[1:4]
        b_cv = banks[4:6]
        b_ig, b_o, b_fill, b_s0, b_s1, b_et, b_pv, b_t = banks
        b_s = [b_s0, b_s1]
        b_w = [b_pv, b_t]
        TC = b_o[0:C, 256:256 + B]

        ld_x, ld_x1, ld_cw, ld_aw, ld_lw, ld_k, ld_v, zeroed = (sem(n) for n in (
            "ld_x", "ld_x1", "ld_cw", "ld_aw", "ld_lw", "ld_k", "ld_v", "zeroed"))
        v_link = sem("v_link")
        p_link = sem("p_link")
        gn_sent, gn_avg, gn_var, gn_rs, xn_done, xc_done = (sem(n) for n in (
            "gn_sent", "gn_avg", "gn_var", "gn_rs", "xn_done", "xc_done"))
        om_mm, om_sb, omt_done, mask_act, mask_done, dist, hat_abs, hat_act, hat_done = (sem(n) for n in (
            "om_mm", "om_sb", "omt_done", "mask_act", "mask_done", "dist", "hat_abs", "hat_act", "hat_done"))
        z_mm, z_sb, a_done, at_mm, at_sb, cv_mm, t0f_done = (sem(n) for n in (
            "z_mm", "z_sb", "a_done", "at_mm", "at_sb", "cv_mm", "t0f_done"))
        t0_mm, t0_sb, ln0_mv, ln0_rs, y_done, yt_mm, yf_done, kv_mm, kv_sb, yb_done = (sem(n) for n in (
            "t0_mm", "t0_sb", "ln0_mv", "ln0_rs", "y_done", "yt_mm", "yf_done", "kv_mm", "kv_sb", "yb_done"))
        q_mm, q_done, s_mm, s_max, e_done, e_inv, e_norm, et_mm, et_sb, pv_mm, o_done = (sem(n) for n in (
            "q_mm", "q_done", "s_mm", "s_max", "e_done", "e_inv", "e_norm", "et_mm", "et_sb", "pv_mm", "o_done"))
        y_mm, r_done, ay_done, h_mm, ge_done, ff_done, ff_mm, t_mv, t_rs, t1_done, ln3_done, xt_mm, xt_done = (
            sem(n) for n in ("y_mm", "r_done", "ay_done", "h_mm", "ge_done", "ff_done", "ff_mm", "t_mv",
                             "t_rs", "t1_done", "ln3_done", "xt_mm", "xt_done"))
        t_link = sem("t_link")
        st_done = sem("st_done")
        tp_link = sem("tp_link")
        lw_done, ig_mm, o_mm, gates, o_gate, u_done, cell, tanh_c, h_done = (sem(n) for n in (
            "lw_done", "ig_mm", "o_mm", "gates", "o_gate", "u_done", "cell", "tanh_c", "h_done"))
        hf_done, out_mm, out_add, stored = (sem(n) for n in ("hf_done", "out_mm", "out_add", "stored"))
        block = ctx.enter_context(nc.Block())

        GROUPS = [(b, k) for b in range(B) for k in range(TAPS)]
        UNITS = [(hg, b) for hg in range(HG) for b in range(B)]
        NU = len(UNITS)
        LAST = NT * STEPS

        def start(m):
            return m * STEPS - LEAD

        def at(g):
            return [(m, g - start(m)) for m in range(NT) if -2 <= g - start(m) < LEAD]

        def leaving(g):
            m, o = divmod(g - OUT_LAG, STEPS)
            return m - 1 if o == 0 and 1 <= m <= NT else None

        EVERY = range(start(0) - 2, LAST + 8)

        @block.sync
        def _(sp):
            sp.dma_start(X2[:], x_fm2).then_inc(ld_x, 16)
            sp.dma_start(CW[:], conv_w).then_inc(ld_cw, 16)
            sp.dma_start(AW[:], attn_w).then_inc(ld_aw, 16)
            sp.dma_start(VEC[:], vecs.rearrange("(o v) c -> o v c", o=1).to_broadcast([P, 5, C])).then_inc(ld_v, 16)
            for m in range(NT):
                sp.wait_ge(out_add, m + 1)
                if m >= 1:
                    sp.wait_ge(stored, 16 * B * m)
                for b in range(B):
                    sp.dma_start(out[b, m * TT:(m + 1) * TT, :], OUT[TT * b:TT * (b + 1), m % 2, :]).then_inc(stored, 16)
            sp.wait_ge(stored, NT * 16 * B)

        @block.gpsimd
        def _(pool):
            def link(ins, n=[0]):
                n[0] += 1
                ins.then_inc(p_link, 1)
                pool.wait_ge(p_link, n[0])

            nc.gpsimd.memset(XN[:], 0.0).then_inc(zeroed, 1)
            nc.gpsimd.memset(half_neg[:], -0.5).then_inc(zeroed, 1)
            nc.gpsimd.memset(H[:], 0.0).then_inc(zeroed, 1)
            nc.gpsimd.memset(VW[:], 0.0).then_inc(zeroed, 1)
            nc.gpsimd.memset(XT[:], 1.0).then_inc(zeroed, 1)
            nc.gpsimd.memset(SA[:], 1.0).then_inc(zeroed, 1)
            nc.gpsimd.memset(CS[:], 0.0).then_inc(zeroed, 1)
            nc.gpsimd.memset(FB[:], 0.0).then_inc(zeroed, 1)
            nc.gpsimd.memset(QB[:], 0.0).then_inc(zeroed, 1)
            pool.wait_ge(zeroed, 9)
            nc.gpsimd.memset(SA[:, :, :, 0], 0.0).then_inc(zeroed, 1)
            pool.wait_ge(gn_var, 1)
            link(nc.gpsimd.tensor_scalar(gvar[:], gvar[:], GN_EPS, None, ALU.add))
            nc.gpsimd.tensor_tensor(grs[:, :, 0], gvar[:, :, 0], half_neg[:, 0:2], ALU.pow).then_inc(gn_rs, 1)
            pool.wait_ge(ld_lw, 16)
            for g, s in ((0, 0.5), (1, 1.0), (2, 0.5)):
                nc.gpsimd.tensor_scalar(VW[0:C, g, :], LW[0:C, LW_V + C * g:LW_V + C * (g + 1)], 0.5 * s, None,
                                        ALU.mult).then_inc(lw_done, 1)
                nc.gpsimd.tensor_scalar(UW[:, g, :], LW[:, LW_U + C * g:LW_U + C * (g + 1)], s, None,
                                        ALU.mult).then_inc(lw_done, 1)
            pool.wait_ge(ln0_mv, NT)
            link(nc.gpsimd.tensor_scalar(rs0[:, :, 0], mv0[:, :, 1], LN_EPS, None, ALU.add))
            nc.gpsimd.tensor_tensor(rs0[:, :, 0], rs0[:, :, 0], half_neg[:], ALU.pow).then_inc(ln0_rs, 1)
            pool.wait_ge(ld_v, 16)
            pool.wait_ge(t0_sb, 1)
            nc.gpsimd.tensor_tensor(TB[:], T0[:], VEC[:, VEC_B2:VEC_B2 + 1, :].to_broadcast([P, NT, C]),
                                    ALU.add).then_inc(yb_done, 1)
            pool.wait_ge(y_done, NT)
            nc.gpsimd.tensor_tensor(YB[:], Y[:], VEC[:, VEC_BO:VEC_BO + 1, :].to_broadcast([P, NT, C]),
                                    ALU.add).then_inc(yb_done, 1)
            for g in EVERY:
                for m, o in at(g):
                    if o in (24, 29, 32):
                        j = (24, 29, 32).index(o)
                        i = 3 * m + j + 1
                        pool.wait_ge(t_mv, i)
                        nc.gpsimd.tensor_scalar(rs[:, j, :], mv[:, j, 1:2], LN_EPS, None, ALU.add).then_inc(tp_link, 1)
                        pool.wait_ge(tp_link, i)
                        nc.gpsimd.tensor_tensor(rs[:, j, :], rs[:, j, :], half_neg[:, 0:1], ALU.pow).then_inc(t_rs, 1)
                if g > 0 and g % STEPS == 0 and g <= LAST:
                    m = g // STEPS - 1
                    if m >= 1:
                        pool.wait_ge(out_mm, m)
                    pool.wait_ge(h_done, g)
                    nc.gpsimd.tensor_copy(HF[:, :, 0:STEPS - 1], H[0:C, 1:STEPS, :].rearrange("p s b -> p b s")
                                          ).then_inc(hf_done, 1)
                    nc.gpsimd.tensor_copy(HF[:, :, STEPS - 1], H[0:C, 0, :]).then_inc(hf_done, 1)

        @block.tensor
        def _(pe):
            pe.wait_ge(ld_k, 16)
            pe.wait_ge(gn_sent, 2)
            nc.tensor.matmul(b_misc[:, 0:4], pair, gme[:].rearrange("p j s -> p (j s)"),
                             start=True, stop=True).then_inc(gn_avg, 1)
            pe.wait_ge(ld_cw, 16)
            pe.wait_ge(xn_done, 2)
            for t in range(TAPS):
                dy, dx = t // 3, t % 3
                mm = nc.tensor.matmul(b_om[0:2 * OFFS, :].rearrange("p (j y x) -> p j y x", j=2, y=SIDE), OW[:, t, :],
                                      XN[:, :, dy:dy + SIDE, dx:dx + SIDE], start=(t == 0), stop=(t == TAPS - 1))
            mm.then_inc(om_mm, 1)

            def z(i):
                b, pt = divmod(i, 2)
                r = slice(C * (b % 2), C * (b % 2) + C)
                if i >= 2:
                    pe.wait_ge(z_sb, 2 * (i - 1))
                for m in range(2):
                    nc.tensor.matmul(b_z[2 * (i % 2) + m][:, 0:288],
                                     XC[r, b // 2, P * pt:P * (pt + 1)], DW[r, 288 * m:288 * (m + 1)],
                                     start=True, stop=True).then_inc(z_mm, 1)

            pe.wait_ge(xc_done, 2)
            z(0)
            z(1)
            pe.wait_ge(om_sb, 1)
            for i in range(4):
                j, h = divmod(i, 2)
                mm = nc.tensor.transpose(b_omt[:, 54 * i:54 * (i + 1)], OM[:, j, P * h:P * (h + 1)],
                                         ident[0:54, 0:54])
            mm.then_inc(omt_done, 1)
            for i in range(2, 2 * B):
                z(i)

            def turn(g):
                pe.wait_ge(a_done, g + 1)
                if g == 0:
                    pe.wait_ge(dist, B)
                    pe.wait_ge(z_sb, 4 * B)
                if g >= 3:
                    pe.wait_ge(at_sb, g - 2)
                for pt in range(2):
                    for h in range(HALVES):
                        q = 2 * pt + h
                        mm = nc.tensor.transpose(b_at[g % 3][:, P * q:P * (q + 1)],
                                                 A[:, g % 4, h, P * pt:P * (pt + 1)], ident)
                mm.then_inc(at_mm, 1)

            def gather(g):
                b, k = GROUPS[g]
                pe.wait_ge(at_sb, g + 1)
                if k == 0 and b >= 2:
                    pe.wait_ge(t0f_done, 2 * (b - 1))
                for pt in range(2):
                    mm = nc.tensor.matmul(b_cv[b % 2][C * pt:C * (pt + 1), 0:N], Z[:, pt, b, k, :],
                                          AT[:, g % 4, pt, :, :], start=(k == 0), stop=(k == TAPS - 1))
                mm.then_inc(cv_mm, 1)

            for g in range(len(GROUPS) + 1):
                if g < len(GROUPS):
                    turn(g)
                if g >= 1:
                    gather(g - 1)

            pe.wait_ge(t0f_done, 2 * B)
            for n in range(NT):
                mm = nc.tensor.transpose(b_misc[:, C * n:C * (n + 1)], T0F[:, n, :, :].rearrange("p b t -> p (b t)"), ident[0:C, 0:C])
            mm.then_inc(t0_mm, 1)
            for i in range(2):
                for n in range(4 * i, 4 * i + 4):
                    pe.wait_ge(y_done, n + 1)
                    mm = nc.tensor.transpose(banks[1 + i][0:C, P * (n % 4):P * (n % 4 + 1)], Y[:, n, :], ident)
                mm.then_inc(yt_mm, 1)
            pe.wait_ge(ld_aw, 16)
            pe.wait_ge(yf_done, 2)
            for i in range(4):
                hg, m = divmod(i, 2)
                nc.tensor.matmul(banks[3 + i][:], AW[0:C, AW_QKV + 256 + P * hg:AW_QKV + 256 + P * (hg + 1)],
                                 YF[:, 2 * m:2 * m + 2, :], start=True, stop=True).then_inc(kv_mm, 1)
            for i in range(4):
                if i == 3:
                    pe.wait_ge(kv_sb, 1)
                bk = [banks[7], banks[1], banks[2], banks[3]][i]
                for h in range(HALVES):
                    mm = nc.tensor.matmul(bk[:, 256 * h:256 * (h + 1)], YF[:, i, P * h:P * (h + 1)],
                                          AW[0:C, AW_QKV + 512:AW_QKV + 768], start=True, stop=True)
                mm.then_inc(kv_mm, 1)
            pe.wait_ge(kv_sb, 8)

            def queries(m):
                if m >= 1:
                    pe.wait_ge(et_sb, NU * m)
                for hg in range(HG):
                    mm = nc.tensor.matmul(b_et[:, P * hg:P * (hg + 1)], AW[0:C, AW_QKV + P * hg:AW_QKV + P * (hg + 1)],
                                          YF[:, :, TT * m:TT * (m + 1)], start=True, stop=True)
                mm.then_inc(q_mm, 1)
                return 4 * HG * P

            def scores(m, u):
                hg, b = UNITS[u]
                i = NU * m + u
                if b == 0:
                    pe.wait_ge(q_done, NU * m + HPG * (hg + 1))
                if i >= 2:
                    pe.wait_ge(e_done, i - 1)
                nc.tensor.matmul(b_s[i % 2][:, 0:N], QB[:, hg, b, :, :].rearrange("p h t -> p (h t)"), KF[:, hg, b, :],
                                 start=True, stop=True).then_inc(s_mm, 1)
                return 4 * N

            def turn_probs(m, u):
                i = NU * m + u
                if u == 0:
                    pe.wait_ge(q_done, NU * (m + 1))
                elif i >= 1:
                    pe.wait_ge(et_sb, i)
                pe.wait_ge(e_norm, i + 1)
                for h in range(HALVES):
                    mm = nc.tensor.transpose(b_et[:, P * h:P * (h + 1)], E[:, i % 2, P * h:P * (h + 1)], ident)
                mm.then_inc(et_mm, 1)
                return 4 * P

            def weigh(m, u):
                hg, b = UNITS[u]
                i = NU * m + u
                pe.wait_ge(et_sb, i + 1)
                if u == 0 and m >= 1:
                    pe.wait_ge(o_done, NU * (m - 1) + HPG)
                if u == B and m >= 1:
                    pe.wait_ge(xt_done, m)
                if u == B and m >= 2:
                    pe.wait_ge(out_add, m - 1)
                for h in range(HALVES):
                    mm = nc.tensor.matmul(b_w[hg][:, P * b:P * (b + 1)], V[:, b, h, P * hg:P * (hg + 1)],
                                          ET[:, i % 2, h, :], start=(h == 0), stop=(h == HALVES - 1),
                                          skip_group_check=True)
                mm.then_inc(pv_mm, 1)
                return 4 * HALVES * P

            def project(m):
                pe.wait_ge(o_done, NU * (m + 1))
                for hg in range(HG):
                    nc.tensor.matmul(b_t[:, 0:C], O[:, hg, :, :].rearrange("p b t -> p (b t)"),
                                     AW[:, AW_OUT + C * hg:AW_OUT + C * (hg + 1)], start=(hg == 0), stop=(hg == HG - 1))
                for hg in range(HG):
                    mm = nc.tensor.matmul(b_t[0:C, P:2 * P], AW[:, AW_OUT + C * hg:AW_OUT + C * (hg + 1)],
                                          O[:, hg, :, :], start=(hg == 0), stop=(hg == HG - 1))
                mm.then_inc(y_mm, 1)
                return 4 * HG * 2 * P

            def widen(m):
                pe.wait_ge(ay_done, m + 1)
                pe.wait_ge(r_done, 2 * m + 1)
                for j in range(2 * FT):
                    mm = nc.tensor.matmul(b_t[:, P * j:P * (j + 1)], AW[0:C, AW_W1 + P * j:AW_W1 + P * (j + 1)],
                                          AY[:], start=True, stop=True)
                mm.then_inc(h_mm, 1)
                return 4 * 2 * FT * P

            def narrow(m):
                pe.wait_ge(ff_done, m + 1)
                for j in range(FT):
                    mm = nc.tensor.matmul(b_t[:, 0:C], FF[:, j, :], AW[:, AW_W2 + C * j:AW_W2 + C * (j + 1)],
                                          start=(j == 0), stop=(j == FT - 1))
                mm.then_inc(ff_mm, 1)
                return 4 * FT * P

            def turn_input(m):
                pe.wait_ge(ln3_done, m + 1)
                nc.tensor.transpose(b_t[0:C, 0:P], LN3[:], ident).then_inc(xt_mm, 1)
                return 2 * P

            def turn_states(m):
                pe.wait_ge(hf_done, 2 * (m + 1))
                pe.wait_ge(xt_done, min(m + 2, NT))
                nc.tensor.transpose(b_t[:, 0:C], HF[:].rearrange("p b s -> p (b s)"), ident[0:C, 0:C]).then_inc(out_mm, 1)
                return 2 * P

            def beside(g):
                cols = 0
                for m, o in at(g):
                    if o == -2:
                        cols += queries(m)
                    if o in range(0, 2 * NU, 2):
                        cols += scores(m, o // 2)
                    if o in range(3, 3 + 2 * NU, 2):
                        cols += turn_probs(m, (o - 3) // 2)
                    if o in range(5, 5 + 2 * NU, 2):
                        cols += weigh(m, (o - 5) // 2)
                    if o == 22:
                        cols += project(m)
                    if o == 24:
                        cols += widen(m)
                    if o == 27:
                        cols += narrow(m)
                    if o == 34:
                        cols += turn_input(m)
                if leaving(g) is not None:
                    cols += turn_states(leaving(g))
                return cols

            def preload(s, gate, dst, width, off, first):
                m, c = divmod(s // CHUNK, STEPS // CHUNK)
                o = dst[0:C, 0:CHUNK * width].rearrange("p (s q) -> p s q", q=width)[:, :, off:off + B]
                r = XT[:, m, :, CHUNK * c:CHUNK * (c + 1)].rearrange("p b s -> p s b")
                nc.tensor.matmul(o, UW[:, gate, :], r, start=first, stop=True, skip_group_check=True)

            def preload_ig(s):
                if s >= 1:
                    pe.wait_ge(gates, s)
                pe.wait_ge(xt_done, s // STEPS + 1)
                preload(s, 0, b_ig, 2 * B, 0, True)
                preload(s, 1, b_ig, 2 * B, B, False)

            def fill(cols):
                while cols >= 128:
                    n = min(cols, 512)
                    nc.tensor.matmul(b_fill[:, 0:n], FB[:, 0:P], FB[:, 0:n], start=True, stop=True)
                    cols -= n

            for g in EVERY:
                if g == 0:
                    pe.wait_ge(lw_done, 6)
                    pe.wait_ge(zeroed, 10)
                    preload_ig(0)
                if 0 <= g < LAST:
                    sc = g % CHUNK
                    if g >= 1:
                        pe.wait_ge(h_done, g)
                    for gate in range(2):
                        mm = nc.tensor.matmul(b_ig[0:C, 8 * sc + 4 * gate:8 * sc + 4 * gate + 4], VW[:, gate, :],
                                              H[:, g % STEPS, :], start=False, stop=True, skip_group_check=True)
                    mm.then_inc(ig_mm, 1)
                    if sc == 0:
                        preload(g, 2, b_o, B, 0, True)
                    nc.tensor.matmul(b_o[0:C, 4 * sc:4 * sc + 4], VW[:, 2, :], H[:, g % STEPS, :], start=False,
                                     stop=True, skip_group_check=True).then_inc(o_mm, 1)
                cols = beside(g)
                if 0 <= g < LAST:
                    if (g + 1) % CHUNK == 0 and g + 1 < LAST:
                        fill(STEP_COLS // 3 - cols)
                        preload_ig(g + 1)
                    else:
                        fill(STEP_COLS - cols)

        @block.scalar
        def _(act):
            act.dma_start(K[:], consts).then_inc(ld_k, 16)
            act.dma_start(X[:], x_fm).then_inc(ld_x1, 16)
            act.dma_start(LW[:], lstm_w).then_inc(ld_lw, 16)

            act.wait_ge(gn_rs, 1)
            act.wait_ge(xn_done, 2)
            for j in range(2):
                nc.scalar.copy(XC[:, j, :].rearrange("p (y x) -> p y x", y=SIDE), XN[:, j, 1:SIDE + 1, 1:SIDE + 1]
                               ).then_inc(xc_done, 1)

            def z_out(i):
                b, pt = divmod(i, 2)
                for m in range(2):
                    act.wait_ge(z_mm, 2 * i + m + 1)
                    nc.scalar.copy(Z[:, pt, b, :, :].rearrange("p k f -> p (k f)")[:, 288 * m:288 * (m + 1)],
                                   b_z[2 * (i % 2) + m][:, 0:288]).then_inc(z_sb, 1)

            act.wait_ge(om_mm, 1)
            nc.scalar.activation(OM[:].rearrange("p j q -> p (j q)"), b_om[0:2 * OFFS, :], ACT.Identity, bias=OB
                                 ).then_inc(om_sb, 1)
            z_out(0)
            z_out(1)
            act.wait_ge(omt_done, 1)
            for i in range(4):
                j, h = divmod(i, 2)
                src = b_omt[:, 54 * i:54 * (i + 1)].rearrange("p (b o) -> p b o", b=2)[:, :, 18:27]
                nc.scalar.activation(MK[:, 2 * j:2 * j + 2, :, h], src, ACT.Tanh, scale=0.5).then_inc(mask_act, 1)
            for b in range(B):
                v = HAT[:, :, b, :, :, :].rearrange("p d k h v -> p d (k h v)")
                act.wait_ge(dist, b + 1)
                nc.scalar.activation(v, v, ACT.Abs).then_inc(hat_abs, 1)
                act.wait_ge(hat_abs, b + 1)
                nc.scalar.activation(v, v, ACT.Relu, bias=1.0, scale=-1.0).then_inc(hat_act, 1)
                if b < 3:
                    z_out(2 * b + 2)
                    z_out(2 * b + 3)
            for g in range(len(GROUPS)):
                act.wait_ge(at_mm, g + 1)
                if g >= 4:
                    act.wait_ge(cv_mm, g - 3)
                nc.scalar.copy(AT[:, g % 4, :, :, :].rearrange("p a h q -> p (a h q)"), b_at[g % 3][:]
                               ).then_inc(at_sb, 1)
            act.wait_ge(t0_mm, 1)
            nc.scalar.copy(T0[:].rearrange("p n c -> p (n c)"), b_misc[:]).then_inc(t0_sb, 1)
            for i in range(2):
                act.wait_ge(yt_mm, i + 1)
                nc.scalar.copy(YF[:, :, P * i:P * (i + 1)].rearrange("p b (n t) -> p n b t", n=4),
                               banks[1 + i][0:C, :].rearrange("p (n b t) -> p n b t", n=4, b=B)).then_inc(yf_done, 1)
            for i in range(8):
                act.wait_ge(kv_mm, i + 1)
                if i < 4:
                    hg, m = divmod(i, 2)
                    nc.scalar.copy(KF[:, hg, 2 * m:2 * m + 2, :].rearrange("p b q -> p (b q)"), banks[3 + i][:]
                                   ).then_inc(kv_sb, 1)
                else:
                    bk = [banks[7], banks[1], banks[2], banks[3]][i - 4]
                    nc.scalar.copy(V[:, i - 4, :, :].rearrange("p h d -> p (h d)"), bk[:]).then_inc(kv_sb, 1)

            def blocks(m, hg):
                act.wait_ge(q_mm, m + 1)
                if m >= 1:
                    act.wait_ge(s_mm, NU * m)
                for h in range(HPG):
                    r = slice(HD * h, HD * (h + 1))
                    nc.scalar.mul(QB[r, hg, :, h, :], b_et[r, P * hg:P * (hg + 1)].rearrange("p (b t) -> p b t", b=B),
                                  HD ** -0.5).then_inc(q_done, 1)

            def exponents(m, u):
                i = NU * m + u
                act.wait_ge(s_max, i + 1)
                if i >= 2:
                    act.wait_ge(et_mm, i - 1)
                nc.scalar.activation(E[:, i % 2, :], b_s[i % 2][:, 0:N], ACT.Exp, bias=nmax[:, i % 2:i % 2 + 1],
                                     accum_out=rsum[:, i % 2:i % 2 + 1]).then_inc(e_done, 1)

            def turned(m, u):
                i = NU * m + u
                act.wait_ge(et_mm, i + 1)
                if i >= 2:
                    act.wait_ge(pv_mm, i - 1)
                nc.scalar.copy(ET[:, i % 2, :, :].rearrange("p h q -> p (h q)"), b_et[:, 0:N]).then_inc(et_sb, 1)

            def gelu(m):
                act.wait_ge(h_mm, m + 1)
                nc.scalar.activation(GE[:].rearrange("p j q -> p (j q)"), b_t[:, 0:FT * P], ACT.Gelu).then_inc(ge_done, 1)

            act.wait_ge(zeroed, 10)
            for g in EVERY:
                if 0 <= g < LAST:
                    sc = g % CHUNK
                    act.wait_ge(ig_mm, g + 1)
                    nc.scalar.activation(SA[:, :, :, 2], b_ig[0:C, 8 * sc:8 * sc + 8].rearrange("p (g b) -> p g b", g=2),
                                         ACT.Tanh).then_inc(gates, 1)
                    act.wait_ge(o_mm, g + 1)
                    nc.scalar.activation(TO[:], b_o[0:C, 4 * sc:4 * sc + 4], ACT.Tanh).then_inc(o_gate, 1)
                    act.wait_ge(cell, g + 1)
                    nc.scalar.activation(TC, CS[:, :, 3], ACT.Tanh, scale=0.5).then_inc(tanh_c, 1)
                for m, o in at(g):
                    if o in (-1, 0):
                        blocks(m, o + 1)
                    if o in range(1, 1 + 2 * NU, 2):
                        exponents(m, (o - 1) // 2)
                    if o in range(4, 4 + 2 * NU, 2):
                        turned(m, (o - 4) // 2)
                    if o == 25:
                        gelu(m)

        @block.vector
        def _(dve):
            def link(ins, n=[0]):
                n[0] += 1
                ins.then_inc(v_link, 1)
                dve.wait_ge(v_link, n[0])

            dve.wait_ge(ld_x, 16)
            for j in range(2):
                ins = nc.vector.bn_stats(gstat[:, j, :], X2[:, j, :])
            link(ins)
            for j in range(2):
                ins = nc.vector.bn_aggr(gmv[:, j, :], gstat[:, j, :])
            link(ins)
            nc.vector.tensor_copy(gme[:, :, 0:1], gmv[:, :, 0:1]).then_inc(gn_sent, 1)
            link(nc.vector.tensor_tensor(gsq[:], gmv[:, :, 0:1], gmv[:, :, 0:1], ALU.mult))
            nc.vector.tensor_tensor(gme[:, :, 1:2], gsq[:], gmv[:, :, 1:2], ALU.add).then_inc(gn_sent, 1)
            dve.wait_ge(gn_avg, 1)
            link(nc.vector.tensor_copy(gmv[:].rearrange("p j s -> p (j s)"), b_misc[:, 0:4]))
            link(nc.vector.tensor_tensor(gsq[:], gmv[:, :, 0:1], gmv[:, :, 0:1], ALU.mult))
            nc.vector.tensor_tensor(gvar[:], gmv[:, :, 1:2], gsq[:], ALU.subtract).then_inc(gn_var, 1)
            dve.wait_ge(zeroed, 1)
            dve.wait_ge(gn_rs, 1)
            for j in range(2):
                nc.vector.tensor_scalar(XN[:, j, 1:SIDE + 1, 1:SIDE + 1],
                                        X2[:, j, :].rearrange("p (y x) -> p y x", y=SIDE),
                                        gmv[:, j, 0:1], grs[:, j, :], ALU.subtract, ALU.mult).then_inc(xn_done, 1)
            dve.wait_ge(ld_k, 16)
            dve.wait_ge(omt_done, 1)
            dve.wait_ge(mask_act, 4)
            for i in range(4):
                j, h = divmod(i, 2)
                src = b_omt[:, 54 * i:54 * (i + 1)].rearrange("p (b o) -> p b o", b=2)[:, :, 0:18].rearrange(
                    "p b (k d) -> p b k d", d=2)
                for bb in range(2):
                    ins = nc.vector.tensor_tensor(POS[:, :, 2 * j + bb, :, h].rearrange("p d k -> p k d"),
                                                  src[:, bb], base[:, h], ALU.add)
            link(ins)
            pos = POS[:].rearrange("p d b k h -> p (d b k h)")
            nc.vector.tensor_scalar(MK[:], MK[:], 0.5, 0.5, ALU.mult, ALU.add)
            link(nc.vector.tensor_scalar(pos, pos, 0.0, float(SIDE + 1), ALU.max, ALU.min))
            for b in range(B):
                kh = TAPS * HALVES
                p_b = POS[:, :, b, :, :].rearrange("p d k h -> p d (k h)")
                nc.vector.tensor_tensor(HAT[:, :, b, :, :, :].rearrange("p d k h v -> p d (k h) v"),
                                        p_b[:, :, :, None].to_broadcast([P, 2, kh, SIDE]),
                                        grid[:, None, None, :].to_broadcast([P, 2, kh, SIDE]),
                                        ALU.subtract).then_inc(dist, 1)

            def masked(b):
                dve.wait_ge(hat_act, b + 1)
                v = HAT[:, 0, b, :, :, :].rearrange("p k h v -> p (k h) v")
                m = MK[:, b, :, :].rearrange("p k h -> p (k h)")
                link(nc.vector.tensor_tensor(v, v, m[:, :, None].to_broadcast([P, TAPS * HALVES, SIDE]), ALU.mult))

            def sampled(b):
                dve.wait_ge(cv_mm, TAPS * (b + 1))
                if b == 0:
                    dve.wait_ge(ld_x1, 16)
                low, high = (b_cv[b % 2][C * i:C * (i + 1), 0:N].rearrange("p (n t) -> p n t", t=TT) for i in range(2))
                nc.vector.tensor_tensor(T0F[:, :, b, :], low, X[:, b, :].rearrange("p (n t) -> p n t", t=TT), ALU.add
                                        ).then_inc(t0f_done, 1)
                dve.wait_ge(t0f_done, 2 * b + 1)
                nc.vector.tensor_tensor(T0F[:, :, b, :], high, T0F[:, :, b, :], ALU.add).then_inc(t0f_done, 1)

            for g, (b, k) in enumerate(GROUPS):
                if k == 0:
                    masked(b)
                if g >= 4:
                    dve.wait_ge(at_mm, g - 3)
                sh = [P, HALVES, SIDE, SIDE]
                nc.vector.tensor_tensor(A[:, g % 4, :, :].rearrange("p h (y x) -> p h y x", y=SIDE),
                                        HAT[:, 0, b, k, :, :, None].to_broadcast(sh),
                                        HAT[:, 1, b, k, :, None, :].to_broadcast(sh), ALU.mult).then_inc(a_done, 1)
                if k == 7 and b >= 1:
                    sampled(b - 1)
            sampled(B - 1)

            dve.wait_ge(t0_sb, 1)
            for n in range(NT):
                ins = nc.vector.bn_stats(st0[:, n, :], T0[:, n, :])
            link(ins)
            for n in range(NT):
                nc.vector.bn_aggr(mv0[:, n, :], st0[:, n, :]).then_inc(ln0_mv, 1)
            dve.wait_ge(ln0_rs, 1)
            for n in range(NT):
                nc.vector.tensor_scalar(Y[:, n, :], T0[:, n, :], mv0[:, n, 0:1], rs0[:, n, :], ALU.subtract,
                                        ALU.mult).then_inc(y_done, 1)
            dve.wait_ge(yb_done, 2)

            def largest(m, u):
                i = NU * m + u
                dve.wait_ge(s_mm, i + 1)
                nc.vector.tensor_reduce(nmax[:, i % 2:i % 2 + 1], b_s[i % 2][:, 0:N], AX.X, ALU.max, negate=True
                                        ).then_inc(s_max, 1)

            def inverse_sum(m, u):
                i = NU * m + u
                dve.wait_ge(e_done, i + 1)
                nc.vector.reciprocal(rinv[:, i % 2:i % 2 + 1], rsum[:, i % 2:i % 2 + 1]).then_inc(e_inv, 1)

            def normalised(m, u):
                i = NU * m + u
                dve.wait_ge(e_inv, i + 1)
                nc.vector.tensor_scalar(E[:, i % 2, :], E[:, i % 2, :], rinv[:, i % 2:i % 2 + 1], None, ALU.mult
                                        ).then_inc(e_norm, 1)

            def head_out(m, hg, h):
                dve.wait_ge(pv_mm, NU * m + B * (hg + 1))
                r = slice(HD * h, HD * (h + 1))
                nc.vector.tensor_copy(O[r, hg, :, :], b_w[hg][r, :].rearrange("p (b h t) -> p b h t", b=B, h=HPG)[:, :, h, :]
                                      ).then_inc(o_done, 1)

            def norm_stats(m, j, src):
                nc.vector.bn_stats(st[:, j, :], src).then_inc(st_done, 1)

            def norm_aggr(m, j):
                dve.wait_ge(st_done, 3 * m + j + 1)
                nc.vector.bn_aggr(mv[:, j, :], st[:, j, :]).then_inc(t_mv, 1)

            def norm_apply(m, j, dst, src):
                dve.wait_ge(t_rs, 3 * m + j + 1)
                return nc.vector.tensor_scalar(dst, src, mv[:, j, 0:1], rs[:, j, :], ALU.subtract, ALU.mult)

            def first(g):
                for m, o in at(g):
                    if o in range(1, 1 + 2 * NU, 2):
                        largest(m, (o - 1) // 2)
                    if o in range(2, 2 + 2 * NU, 2):
                        inverse_sum(m, (o - 2) // 2)
                    if o == 23:
                        dve.wait_ge(y_mm, m + 1)
                        nc.vector.tensor_scalar(AY[:], b_t[0:C, P:2 * P], AW[0:C, AW_BO:AW_BO + 1], None, ALU.add
                                                ).then_inc(ay_done, 1)
                    if o == 25:
                        norm_apply(m, 0, X1[:], R1[:]).then_inc(t_link, 1)
                    if o == 26:
                        dve.wait_ge(ge_done, m + 1)
                        nc.vector.tensor_tensor(FF[:].rearrange("p j q -> p (j q)"), b_t[:, FT * P:2 * FT * P],
                                                GE[:].rearrange("p j q -> p (j q)"), ALU.mult).then_inc(ff_done, 1)
                    if o == 28:
                        dve.wait_ge(ff_mm, m + 1)
                        dve.wait_ge(t_link, 5 * m + 3)
                        nc.vector.tensor_tensor(R2[:], b_t[:, 0:C], X1[:], ALU.add).then_inc(r_done, 1)
                    if o == 30:
                        norm_apply(m, 1, R2[:], R2[:]).then_inc(t_link, 1)
                    if o == 31:
                        dve.wait_ge(t_link, 5 * m + 5)
                        nc.vector.tensor_tensor(T1[:, m, :], R2[:], TB[:, m, :], ALU.add).then_inc(t1_done, 1)
                    if o == 33:
                        norm_apply(m, 2, LN3[:], T1[:, m, :]).then_inc(ln3_done, 1)
                    if o == 36:
                        dve.wait_ge(xt_mm, m + 1)
                        nc.vector.tensor_copy(XT[0:C, m, :, :].rearrange("p b t -> p (b t)"), b_t[0:C, 0:P]
                                              ).then_inc(xt_done, 1)
                if leaving(g - 1) is not None:
                    m = leaving(g - 1)
                    dve.wait_ge(out_mm, m + 1)
                    if m >= 2:
                        dve.wait_ge(stored, 16 * B * (m - 1))
                    nc.vector.scalar_tensor_tensor(out=OUT[:, m % 2, :], in0=b_t[:, 0:C], scalar=0.5, in1=T1[:, m, :],
                                                   op0=ALU.mult, op1=ALU.add).then_inc(out_add, 1)

            def second(g):
                for m, o in at(g):
                    if o in range(2, 2 + 2 * NU, 2):
                        normalised(m, (o - 2) // 2)
                    if o == 20:
                        head_out(m, 1, 0)
                        head_out(m, 1, 1)
                    if o == 21:
                        head_out(m, 1, 3)
                    if o == 23:
                        nc.vector.tensor_tensor(R1[:], b_t[:, 0:C], YB[:, m, :], ALU.add).then_inc(r_done, 1)
                    if o == 24:
                        norm_aggr(m, 0)
                    if o == 29:
                        norm_aggr(m, 1)
                    if o == 32:
                        norm_aggr(m, 2)

            def third(g):
                for m, o in at(g):
                    if o in range(12, 12 + HPG):
                        head_out(m, 0, o - 12)
                    if o == 20:
                        head_out(m, 1, 2)
                    if o == 23:
                        dve.wait_ge(r_done, 2 * m + 1)
                        norm_stats(m, 0, R1[:])
                    if o == 25:
                        dve.wait_ge(t_link, 5 * m + 1)
                        nc.vector.tensor_tensor(X1[:], X1[:], VEC[:, VEC_G1, :], ALU.mult).then_inc(t_link, 1)
                    if o == 26:
                        dve.wait_ge(t_link, 5 * m + 2)
                        nc.vector.tensor_tensor(X1[:], X1[:], VEC[:, VEC_B1, :], ALU.add).then_inc(t_link, 1)
                    if o == 28:
                        dve.wait_ge(r_done, 2 * m + 2)
                        norm_stats(m, 1, R2[:])
                    if o == 30:
                        dve.wait_ge(t_link, 5 * m + 4)
                        nc.vector.tensor_tensor(R2[:], R2[:], VEC[:, VEC_G2, :], ALU.mult).then_inc(t_link, 1)
                    if o == 31:
                        dve.wait_ge(t1_done, m + 1)
                        norm_stats(m, 2, T1[:, m, :])

            for g in EVERY:
                cell_step = 0 <= g < LAST
                first(g)
                if cell_step:
                    if g >= 1:
                        dve.wait_ge(h_done, g)
                    nc.vector.scalar_tensor_tensor(out=SA[:, 0, :, 3], in0=H[0:C, g % STEPS, :], scalar=0.5,
                                                   in1=CS[:, :, 3], op0=ALU.mult, op1=ALU.mult).then_inc(u_done, 1)
                second(g)
                if cell_step:
                    dve.wait_ge(gates, g + 1)
                    dve.wait_ge(u_done, g + 1)
                    nc.vector.tensor_tensor_scan(CS[:].rearrange("p b q -> p (b q)"),
                                                 SA[:, 0, :, :].rearrange("p b q -> p (b q)"),
                                                 SA[:, 1, :, :].rearrange("p b q -> p (b q)"), 0.0,
                                                 op0=ALU.add, op1=ALU.mult).then_inc(cell, 1)
                third(g)
                if cell_step:
                    dve.wait_ge(tanh_c, g + 1)
                    dve.wait_ge(o_gate, g + 1)
                    if g % STEPS == 0 and g >= STEPS:
                        dve.wait_ge(hf_done, 2 * (g // STEPS))
                    nc.vector.scalar_tensor_tensor(out=H[0:C, (g + 1) % STEPS, :], in0=TO[:], scalar=1.0, in1=TC,
                                                   op0=ALU.add, op1=ALU.mult).then_inc(h_done, 1)


def shape_constants():
    k = np.zeros((P, K_END), np.float32)
    p = np.arange(P)
    k[p, K_ID + p] = 1.0
    k[:, K_PAIR:K_PAIR + P] = np.where(p[:, None] // 2 == p[None, :] // 2, 0.5, 0.0)
    k[:, K_MASK:K_MASK + HPG] = np.where(p[:, None] // HD == np.arange(HPG)[None, :], HD ** -0.5, 0.0)
    base = np.zeros((P, HALVES, TAPS, 2), np.float32)
    for h in range(HALVES):
        for t in range(TAPS):
            base[:, h, t, 0] = (P * h + p) // SIDE + 1 + t // 3 - 1
            base[:, h, t, 1] = p % SIDE + 1 + t % 3 - 1
    k[:, K_BASE:K_BASE + 36] = base.reshape(P, 36)
    k[:, K_GRID:K_GRID + SIDE] = np.arange(1, SIDE + 1)
    return k


def packed(i):
    f = {n: np.asarray(a) for n, a in i.items()}
    x = f["x"].reshape(B // 2, 2, N, C)
    a = {}
    a["x_fm2"] = np.ascontiguousarray(x.transpose(1, 3, 0, 2).reshape(P, 2, N))
    a["x_fm"] = np.ascontiguousarray(f["x"].reshape(B, N, C).transpose(2, 0, 1))
    cw = np.zeros((P, CW_END), np.float32)
    ow = f["L0_conv_offset_w"].reshape(TAPS, C, OFFS).transpose(1, 0, 2)
    dw = f["L0_conv_dcn_weight"].transpose(1, 2, 3, 0).reshape(C, TAPS * C)
    for h in range(2):
        r = slice(C * h, C * (h + 1))
        cw[r, 0:CW_DW].reshape(C, TAPS, 2, OFFS)[:, :, h, :] = ow
        cw[r, CW_DW:CW_OB] = dw
        cw[OFFS * h:OFFS * (h + 1), CW_OB] = f["L0_conv_offset_b"].reshape(OFFS)
    a["conv_w"] = cw
    aw = np.zeros((P, AW_END), np.float32)
    aw[0:C, AW_QKV:AW_OUT] = f["L1_attn_w_qkv"].T
    aw[:, AW_OUT:AW_W1] = f["L1_attn_w_out"].T.reshape(HG, P, C).transpose(1, 0, 2).reshape(P, HG * C)
    aw[0:C, AW_W1:AW_WV] = f["L1_attn_w1"].T
    aw[0:C, AW_WV:AW_W2] = f["L1_attn_wv"].T
    aw[:, AW_W2:AW_BO] = f["L1_attn_w2"].T.reshape(FT, P, C).transpose(1, 0, 2).reshape(P, FT * C)
    aw[0:C, AW_BO] = f["L1_attn_b_out"]
    a["attn_w"] = aw
    lw = np.zeros((C + 1, LW_END), np.float32)
    for j, g in enumerate("ico"):
        lw[0:C, LW_V + C * j:LW_V + C * (j + 1)] = f[f"L1_ffn_V_{g}"]
        lw[0:C, LW_U + C * j:LW_U + C * (j + 1)] = f[f"L1_ffn_U_{g}"]
        lw[C, LW_U + C * j:LW_U + C * (j + 1)] = f[f"L1_ffn_b_{g}"]
    a["lstm_w"] = lw
    a["vecs"] = np.stack([f[f"L1_attn_{n}"] for n in ("b_out", "ln1_g", "ln1_b", "ln2_g", "ln2_b")])
    a["consts"] = shape_constants()
    return a


def kernel(**inputs):
    import concourse.bacc as _bacc
    from concourse.bass_utils import run_bass_kernel_spmd as _run

    nc = _bacc.Bacc("TRN2", target_bir_lowering=False, num_devices=1)
    arrays = packed(inputs)
    args = [nc.dram_tensor(f"in_{n}", a.shape, F32, kind="ExternalInput").ap() for n, a in arrays.items()]
    out = nc.dram_tensor("out_0_dram", (B, N, C), F32, kind="ExternalOutput").ap()
    hybrid_kernel(nc, *args, out)
    r = _run(nc, [{f"in_{n}": a for n, a in arrays.items()}], core_ids=[0])
    return r.results[0]["out_0_dram"].reshape(B, SIDE, SIDE, C)
```

```python
from contextlib import ExitStack

import numpy as np

import concourse.bass as bass
from concourse import mybir

F32 = mybir.dt.float32
BF16 = mybir.dt.bfloat16
ALU = mybir.AluOpType
ACT = mybir.ActivationFunctionType
AX = mybir.AxisListType

P = 128
B, SIDE, C = 4, 16, 64
N = SIDE * SIDE
TAPS = 9
OFFS = 3 * TAPS
HALVES = N // P
HEADS, HD = 8, 32
HG = HEADS * HD // P
HPG = HEADS // HG
DFF = 256
FT = DFF // P
TT = 32
NT = N // TT
STEPS = TT
HC = C // 2
CHUNK = 16
LEAD = 38
HATS_AT = 3
FIRST = -5
OUT_LAG = 2
GN_EPS = LN_EPS = 1e-5
COLS_LOAD = 5120
COLS_GROUPS = 4096
COLS_LN = 5632
COLS_TURN = 256
COLS_TURNED = 2048
COLS_EARLY = 800
COLS_STEP = 1800
COLS_TABLE = 1500

K_ID, K_PAIR, K_MASK, K_BASE, K_GRID = 0, 128, 256, 260, 296
K_END = 312
CW_OW, CW_OB = 0, TAPS * 2 * OFFS
CW_END = CW_OB + 1
AW_QKV, AW_OUT, AW_W1, AW_WV = 0, 768, 768 + HG * C, 768 + HG * C + DFF
AW_W2 = AW_WV + DFF
AW_BO = AW_W2 + FT * C
AW_END = AW_BO + 1
LW_V, LW_U, LW_END = 0, 3 * C, 6 * C
VEC_BO, VEC_G1, VEC_B1, VEC_G2, VEC_B2 = range(5)


def hybrid_kernel(nc, x_fm2, x_fm, conv_w, dcn_w, attn_w, lstm_w, vecs, consts, out):
    ctx = ExitStack()
    with ctx:
        def sb(name, shape, dt=F32):
            return ctx.enter_context(nc.sbuf_tensor(name, shape, dt))

        def bank(name):
            return ctx.enter_context(nc.psum_tensor(name, [P, 512], F32))

        def sem(name):
            return ctx.enter_context(nc.semaphore(name))

        X2 = sb("X2", [P, 2, N])
        X = sb("X", [C, B, N])
        CW = sb("CW", [P, CW_END])
        DW = sb("DW", [P, 2, TAPS * C])
        AW = sb("AW", [P, AW_END])
        LW = sb("LW", [C + 1, LW_END])
        VEC = sb("VEC", [P, 5, C])
        K = sb("K", [P, K_END])
        ident = K[:, K_ID:K_ID + P]
        pair = K[:, K_PAIR:K_PAIR + P]
        head_mask = K[:, K_MASK:K_MASK + HPG]
        base = K[:, K_BASE:K_BASE + 36].rearrange("p (h k d) -> p h k d", h=2, d=2)
        grid = K[:, K_GRID:K_GRID + SIDE]
        OW = CW[:, CW_OW:CW_OB].rearrange("p (t o) -> p t o", t=TAPS)
        OB = CW[0:2 * OFFS, CW_OB:CW_OB + 1]

        gstat = sb("gstat", [P, 2, 6])
        gmv = sb("gmv", [P, 2, 2])
        gsq = sb("gsq", [P, 2, 1])
        gme = sb("gme", [P, 2, 2])
        gvar = sb("gvar", [P, 2, 1])
        grs = sb("grs", [P, 2, 1])
        XN = sb("XN", [P, 2, SIDE + 2, SIDE + 2])
        XC = sb("XC", [P, 2, N])
        OM = sb("OM", [2 * OFFS, 2, N])
        POS = sb("POS", [P, 2, B, TAPS, HALVES])
        MK = sb("MK", [P, B, TAPS, HALVES])
        HAT = sb("HAT", [P, 2, B, TAPS, HALVES, SIDE])
        A = sb("A", [P, 4, HALVES, N])
        AT = sb("AT", [P, 4, 2, HALVES, P])
        Z = sb("Z", [P, 2, B, TAPS, C])
        T0F = sb("T0F", [C, NT, B, TT])
        T0 = sb("T0", [P, NT, C])
        st0 = sb("st0", [P, NT, 6])
        mv0 = sb("mv0", [P, NT, 2])
        rs0 = sb("rs0", [P, NT, 1])
        Y = sb("Y", [P, NT, C])
        YB = sb("YB", [P, NT, C])
        TB = sb("TB", [P, NT, C])
        YF = sb("YF", [P, B, N])
        KF = sb("KF", [P, HG, B, N])
        V = sb("V", [P, B, HALVES, HEADS * HD])
        QB = sb("QB", [P, HG, B, HPG, TT])
        nmax = sb("nmax", [P, 2])
        rsum = sb("rsum", [P, 2])
        rinv = sb("rinv", [P, 2])
        E = sb("E", [P, 2, N])
        ET = sb("ET", [P, 2, HALVES, P])
        O = sb("O", [P, HG, B, TT])
        AY = sb("AY", [P, P])
        R1 = sb("R1", [P, C])
        R2 = sb("R2", [P, C])
        X1 = sb("X1", [P, C])
        GE = sb("GE", [P, FT, P])
        FF = sb("FF", [P, FT, P])
        st = sb("st", [P, 3, 6])
        mv = sb("mv", [P, 3, 2])
        rs = sb("rs", [P, 3, 1])
        half_neg = sb("half_neg", [P, NT])
        T1 = sb("T1", [P, NT, C])
        LN3 = sb("LN3", [P, C])
        XT = sb("XT", [C + 1, NT, B, TT])
        VW = sb("VW", [P, 3, C])
        UW = sb("UW", [C + 1, 3, C])
        H = sb("H", [P, STEPS, B])
        HF = sb("HF", [C, B, TT])
        SA = sb("SA", [C, 2, B, 4])
        TO = sb("TO", [C, B])
        OUT = sb("OUT", [P, 2, C])
        scrap = sb("scrap", [1, 1])
        FB = sb("FB", [P, 512], BF16)

        banks = [bank(f"bank{i}") for i in range(8)]
        b_misc, b_om, b_omt = banks[0], banks[1], banks[2]
        b_z = banks[3:8] + banks[0:1]
        b_at = banks[1:4]
        b_cv = banks[4:6]
        b_t0 = (banks[0], banks[6])
        b_ig, b_o, b_fill, b_s0, b_s1, b_et, b_pv, b_t = banks
        b_s = [b_s0, b_s1]
        b_v = [b_t, b_ig, b_o, b_pv]
        b_w = [b_pv, b_t]
        CS = b_o[C:P, 0:4 * B].rearrange("p (b q) -> p b q", q=4)
        TC = b_o[C:P, 4 * B:5 * B]

        ld_x, ld_x1, ld_cw, ld_aw, ld_lw, ld_k, ld_v, zeroed = (sem(n) for n in (
            "ld_x", "ld_x1", "ld_cw", "ld_aw", "ld_lw", "ld_k", "ld_v", "zeroed"))
        v_link = sem("v_link")
        p_link = sem("p_link")
        gn_sent, gn_avg, gn_var, gn_rs, xn_done, xc_done = (sem(n) for n in (
            "gn_sent", "gn_avg", "gn_var", "gn_rs", "xn_done", "xc_done"))
        om_mm, om_sb, omt_done, mask_act, mask_done, dist, hat_abs, hat_act, hat_done = (sem(n) for n in (
            "om_mm", "om_sb", "omt_done", "mask_act", "mask_done", "dist", "hat_abs", "hat_act", "hat_done"))
        z_mm, z_sb, a_done, at_mm, at_sb, cv_mm, t0f_done = (sem(n) for n in (
            "z_mm", "z_sb", "a_done", "at_mm", "at_sb", "cv_mm", "t0f_done"))
        t0_mm, t0_sb, ln0_mv, ln0_rs, y_done, yt_mm, yf_done, k_mm, k_sb, v_mm, v_sb, yb_done = (sem(n) for n in (
            "t0_mm", "t0_sb", "ln0_mv", "ln0_rs", "y_done", "yt_mm", "yf_done", "k_mm", "k_sb", "v_mm", "v_sb", "yb_done"))
        q_mm, q_done, s_mm, s_max, e_done, e_inv, e_norm, et_mm, et_sb, pv_mm, o_done = (sem(n) for n in (
            "q_mm", "q_done", "s_mm", "s_max", "e_done", "e_inv", "e_norm", "et_mm", "et_sb", "pv_mm", "o_done"))
        y_mm, r_done, ay_done, h_mm, ge_done, ff_done, ff_mm, t_mv, t_rs, t1_done, ln3_done, xt_mm, xt_done = (
            sem(n) for n in ("y_mm", "r_done", "ay_done", "h_mm", "ge_done", "ff_done", "ff_mm", "t_mv",
                             "t_rs", "t1_done", "ln3_done", "xt_mm", "xt_done"))
        t_link = sem("t_link")
        st_done = sem("st_done")
        tp_link = sem("tp_link")
        lw_done, ig_mm, o_mm, gates, o_gate, u_done, cell, tanh_c, h_done = (sem(n) for n in (
            "lw_done", "ig_mm", "o_mm", "gates", "o_gate", "u_done", "cell", "tanh_c", "h_done"))
        cs_zero = sem("cs_zero")
        ln0_st = sem("ln0_st")
        om_low = sem("om_low")
        ld_dw, fb_zero = sem("ld_dw"), sem("fb_zero")
        hf_done, out_mm, out_add, stored = (sem(n) for n in ("hf_done", "out_mm", "out_add", "stored"))
        block = ctx.enter_context(nc.Block())

        GROUPS = [(b, k) for b in range(B) for k in range(TAPS)]
        UNITS = [(hg, b) for hg in range(HG) for b in range(B)]
        NU = len(UNITS)
        LAST = NT * STEPS

        def start(m):
            return m * STEPS - LEAD

        def at(g):
            return [(m, g - start(m)) for m in range(NT) if FIRST <= g - start(m) < LEAD]

        def leaving(g):
            m, o = divmod(g - OUT_LAG, STEPS)
            return m - 1 if o == 0 and 1 <= m <= NT else None

        EVERY = range(start(0) + FIRST, LAST + OUT_LAG + 2)

        @block.sync
        def _(sp):
            sp.dma_start(X2[:], x_fm2).then_inc(ld_x, 16)
            sp.dma_start(CW[:], conv_w).then_inc(ld_cw, 16)
            sp.dma_start(DW[:], dcn_w).then_inc(ld_dw, 16)
            sp.dma_start(AW[:], attn_w).then_inc(ld_aw, 16)
            sp.dma_start(VEC[:], vecs.rearrange("(o v) c -> o v c", o=1).to_broadcast([P, 5, C])).then_inc(ld_v, 16)
            for m in range(NT):
                sp.wait_ge(out_add, m + 1)
                if m >= 1:
                    sp.wait_ge(stored, 16 * m)
                sp.dma_start(out[m], OUT[:, m % 2, :]).then_inc(stored, 16)
            sp.wait_ge(stored, NT * 16)

        @block.gpsimd
        def _(pool):
            def link(ins, n=[0]):
                n[0] += 1
                ins.then_inc(p_link, 1)
                pool.wait_ge(p_link, n[0])

            nc.gpsimd.memset(XN[:], 0.0).then_inc(zeroed, 1)
            nc.gpsimd.memset(half_neg[:], -0.5).then_inc(zeroed, 1)
            nc.gpsimd.memset(H[:], 0.0).then_inc(zeroed, 1)
            nc.gpsimd.memset(VW[:], 0.0).then_inc(zeroed, 1)
            nc.gpsimd.memset(XT[:], 1.0).then_inc(zeroed, 1)
            nc.gpsimd.memset(SA[:], 1.0).then_inc(zeroed, 1)
            nc.gpsimd.memset(YF[:], 0.0).then_inc(zeroed, 1)
            nc.gpsimd.memset(AY[:], 0.0).then_inc(zeroed, 1)
            nc.gpsimd.memset(QB[:], 0.0).then_inc(zeroed, 1)
            pool.wait_ge(zeroed, 9)
            nc.gpsimd.memset(SA[:, :, :, 0], 0.0).then_inc(zeroed, 1)
            pool.wait_ge(gn_var, 1)
            link(nc.gpsimd.tensor_scalar(gvar[:], gvar[:], GN_EPS, None, ALU.add))
            nc.gpsimd.tensor_tensor(grs[:, :, 0], gvar[:, :, 0], half_neg[:, 0:2], ALU.pow).then_inc(gn_rs, 1)
            pool.wait_ge(ld_lw, 16)
            for g, s in ((0, 0.5), (1, 1.0), (2, 0.5)):
                nc.gpsimd.tensor_scalar(VW[0:C, g, :], LW[0:C, LW_V + C * g:LW_V + C * (g + 1)], 0.5 * s, None,
                                        ALU.mult).then_inc(lw_done, 1)
                nc.gpsimd.tensor_scalar(UW[:, g, :], LW[:, LW_U + C * g:LW_U + C * (g + 1)], s, None,
                                        ALU.mult).then_inc(lw_done, 1)
            for i in range(2):
                half = slice(4 * i, 4 * i + 4)
                pool.wait_ge(ln0_mv, 4 * (i + 1))
                link(nc.gpsimd.tensor_scalar(rs0[:, half, 0], mv0[:, half, 1], LN_EPS, None, ALU.add))
                nc.gpsimd.tensor_tensor(rs0[:, half, 0], rs0[:, half, 0], half_neg[:, half], ALU.pow).then_inc(ln0_rs, 1)
            pool.wait_ge(ld_v, 16)
            pool.wait_ge(t0_sb, 2)
            nc.gpsimd.tensor_tensor(TB[:], T0[:], VEC[:, VEC_B2:VEC_B2 + 1, :].to_broadcast([P, NT, C]),
                                    ALU.add).then_inc(yb_done, 1)
            pool.wait_ge(y_done, NT)
            nc.gpsimd.tensor_tensor(YB[:], Y[:], VEC[:, VEC_BO:VEC_BO + 1, :].to_broadcast([P, NT, C]),
                                    ALU.add).then_inc(yb_done, 1)
            for g in EVERY:
                for m, o in at(g):
                    if o in (24, 29, 32):
                        j = (24, 29, 32).index(o)
                        i = 3 * m + j + 1
                        pool.wait_ge(t_mv, i)
                        nc.gpsimd.tensor_scalar(rs[:, j, :], mv[:, j, 1:2], LN_EPS, None, ALU.add).then_inc(tp_link, 1)
                        pool.wait_ge(tp_link, i)
                        nc.gpsimd.tensor_tensor(rs[:, j, :], rs[:, j, :], half_neg[:, 0:1], ALU.pow).then_inc(t_rs, 1)
                if g > 0 and g % STEPS == 0 and g < LAST:
                    m = g // STEPS - 1
                    if m >= 1:
                        pool.wait_ge(out_mm, m)
                    pool.wait_ge(h_done, g)
                    nc.gpsimd.tensor_copy(HF[:, :, 0:STEPS - 1], H[0:C, 1:STEPS, :].rearrange("p s b -> p b s")
                                          ).then_inc(hf_done, 1)
                    nc.gpsimd.tensor_copy(HF[:, :, STEPS - 1], H[0:C, 0, :]).then_inc(hf_done, 1)

        @block.tensor
        def _(pe):
            def fill(cols, idle):
                while cols >= 128:
                    n = min(cols, 512)
                    nc.tensor.matmul(idle[:, 0:n], FB[:, 0:P], FB[:, 0:n], start=True, stop=True)
                    cols -= n

            pe.wait_ge(fb_zero, 1)
            fill(COLS_LOAD, banks[7])
            pe.wait_ge(ld_k, 16)
            pe.wait_ge(gn_sent, 2)
            nc.tensor.matmul(b_misc[:, 0:4], pair, gme[:].rearrange("p j s -> p (j s)"),
                             start=True, stop=True).then_inc(gn_avg, 1)
            fill(COLS_GROUPS, banks[7])
            pe.wait_ge(ld_cw, 16)
            pe.wait_ge(xn_done, 2)
            for t in range(TAPS):
                dy, dx = t // 3, t % 3
                r = slice(C * (t % 2), C * (t % 2) + 2 * OFFS)
                mm = nc.tensor.matmul(b_om[r, :].rearrange("p (j y x) -> p j y x", j=2, y=SIDE), OW[:, t, :],
                                      XN[:, :, dy:dy + SIDE, dx:dx + SIDE], start=(t < 2), stop=(t >= TAPS - 2))
            mm.then_inc(om_mm, 1)

            def z(i):
                b, pt = divmod(i, 2)
                if i >= 3:
                    pe.wait_ge(z_sb, 2 * (i - 2))
                for m in range(2):
                    nc.tensor.matmul(b_z[2 * (i % 3) + m][:, 0:288],
                                     XC[:, b // 2, P * pt:P * (pt + 1)], DW[:, b % 2, 288 * m:288 * (m + 1)],
                                     start=True, stop=True).then_inc(z_mm, 1)

            pe.wait_ge(ld_dw, 16)
            pe.wait_ge(xc_done, 2)
            z(0)
            for i in range(4):
                j, h = divmod(i, 2)
                if h == 0:
                    pe.wait_ge(om_sb, j + 1)
                mm = nc.tensor.transpose(b_omt[:, 54 * i:54 * (i + 1)], OM[:, j, P * h:P * (h + 1)],
                                         ident[0:54, 0:54])
            mm.then_inc(omt_done, 1)
            for i in range(1, 2 * B):
                z(i)

            def turn(g):
                pe.wait_ge(a_done, g + 1)
                if g == 0:
                    pe.wait_ge(dist, 1)
                if g >= 3:
                    pe.wait_ge(at_sb, g - 2)
                for pt in range(2):
                    for h in range(HALVES):
                        q = 2 * pt + h
                        mm = nc.tensor.transpose(b_at[g % 3][:, P * q:P * (q + 1)],
                                                 A[:, g % 4, h, P * pt:P * (pt + 1)], ident)
                mm.then_inc(at_mm, 1)

            def gather(g):
                b, k = GROUPS[g]
                pe.wait_ge(at_sb, g + 1)
                if g == 0:
                    pe.wait_ge(z_sb, 4 * B)
                if k == 0 and b >= 2:
                    pe.wait_ge(t0f_done, 2 * (b - 1))
                for pt in range(2):
                    mm = nc.tensor.matmul(b_cv[b % 2][C * pt:C * (pt + 1), 0:N], Z[:, pt, b, k, :],
                                          AT[:, g % 4, pt, :, :], start=(k == 0), stop=(k == TAPS - 1))
                mm.then_inc(cv_mm, 1)

            for g in range(len(GROUPS) + 1):
                if g < len(GROUPS):
                    turn(g)
                if g >= 1:
                    gather(g - 1)

            pe.wait_ge(t0f_done, 2 * B)
            for n in range(NT):
                mm = nc.tensor.transpose(b_t0[n // 4][:, C * (n % 4):C * (n % 4 + 1)], T0F[:, n, :, :].rearrange("p b t -> p (b t)"), ident[0:C, 0:C])
                if n % 4 == 3:
                    mm.then_inc(t0_mm, 1)
            fill(COLS_LN, banks[7])
            for i in range(2):
                for n in range(4 * i, 4 * i + 4):
                    pe.wait_ge(y_done, n + 1)
                    mm = nc.tensor.transpose(banks[1 + i][0:C, P * (n % 4):P * (n % 4 + 1)], Y[:, n, :], ident)
                    fill(COLS_TURN, banks[7])
                mm.then_inc(yt_mm, 1)
            fill(COLS_TURNED, banks[7])
            pe.wait_ge(ld_aw, 16)
            pe.wait_ge(zeroed, 10)
            pe.wait_ge(yf_done, 2)
            for i in range(4):
                hg, m = divmod(i, 2)
                nc.tensor.matmul(banks[3 + i][:], AW[:, AW_QKV + 256 + P * hg:AW_QKV + 256 + P * (hg + 1)],
                                 YF[:, 2 * m:2 * m + 2, :], start=True, stop=True).then_inc(k_mm, 1)

            def values(b):
                if b == 3:
                    pe.wait_ge(k_sb, 4)
                for h in range(HALVES):
                    mm = nc.tensor.matmul(b_v[b][:, 256 * h:256 * (h + 1)], YF[:, b, P * h:P * (h + 1)],
                                          AW[:, AW_QKV + 512:AW_QKV + 768], start=True, stop=True)
                mm.then_inc(v_mm, 1)

            def queries(m):
                if m >= 1:
                    pe.wait_ge(et_sb, NU * m)
                else:
                    pe.wait_ge(k_sb, 3)
                for hg in range(HG):
                    mm = nc.tensor.matmul(b_et[:, P * hg:P * (hg + 1)], AW[:, AW_QKV + P * hg:AW_QKV + P * (hg + 1)],
                                          YF[:, :, TT * m:TT * (m + 1)], start=True, stop=True)
                mm.then_inc(q_mm, 1)
                return 4 * HG * P

            def scores(m, u):
                hg, b = UNITS[u]
                i = NU * m + u
                if b == 0:
                    pe.wait_ge(q_done, NU * m + HPG * (hg + 1))
                if i >= 2:
                    pe.wait_ge(e_done, i - 1)
                else:
                    pe.wait_ge(k_sb, 4)
                nc.tensor.matmul(b_s[i % 2][:, 0:N], QB[:, hg, b, :, :].rearrange("p h t -> p (h t)"), KF[:, hg, b, :],
                                 start=True, stop=True).then_inc(s_mm, 1)
                return 4 * N

            def turn_probs(m, u):
                i = NU * m + u
                if u == 0:
                    pe.wait_ge(q_done, NU * (m + 1))
                elif i >= 1:
                    pe.wait_ge(et_sb, i)
                pe.wait_ge(e_norm, i + 1)
                for h in range(HALVES):
                    mm = nc.tensor.transpose(b_et[:, P * h:P * (h + 1)], E[:, i % 2, P * h:P * (h + 1)], ident)
                mm.then_inc(et_mm, 1)
                return 4 * P

            def weigh(m, u):
                hg, b = UNITS[u]
                i = NU * m + u
                pe.wait_ge(et_sb, i + 1)
                if i < B:
                    pe.wait_ge(v_sb, B)
                if u == 0 and m >= 1:
                    pe.wait_ge(o_done, NU * (m - 1) + HPG)
                if u == B and m >= 1:
                    pe.wait_ge(xt_done, m)
                if u == B and m >= 2:
                    pe.wait_ge(out_add, m - 1)
                for h in range(HALVES):
                    mm = nc.tensor.matmul(b_w[hg][:, P * b:P * (b + 1)], V[:, b, h, P * hg:P * (hg + 1)],
                                          ET[:, i % 2, h, :], start=(h == 0), stop=(h == HALVES - 1),
                                          skip_group_check=True)
                mm.then_inc(pv_mm, 1)
                return 4 * HALVES * P

            def project(m):
                pe.wait_ge(o_done, NU * (m + 1))
                for hg in range(HG):
                    nc.tensor.matmul(b_t[:, 0:C], O[:, hg, :, :].rearrange("p b t -> p (b t)"),
                                     AW[:, AW_OUT + C * hg:AW_OUT + C * (hg + 1)], start=(hg == 0), stop=(hg == HG - 1))
                for hg in range(HG):
                    mm = nc.tensor.matmul(b_t[0:C, P:2 * P], AW[:, AW_OUT + C * hg:AW_OUT + C * (hg + 1)],
                                          O[:, hg, :, :], start=(hg == 0), stop=(hg == HG - 1))
                mm.then_inc(y_mm, 1)
                return 4 * HG * 2 * P

            def widen(m):
                pe.wait_ge(ay_done, m + 1)
                pe.wait_ge(r_done, 2 * m + 1)
                for j in range(2 * FT):
                    mm = nc.tensor.matmul(b_t[:, P * j:P * (j + 1)], AW[:, AW_W1 + P * j:AW_W1 + P * (j + 1)],
                                          AY[:], start=True, stop=True)
                mm.then_inc(h_mm, 1)
                return 4 * 2 * FT * P

            def narrow(m):
                pe.wait_ge(ff_done, m + 1)
                for j in range(FT):
                    mm = nc.tensor.matmul(b_t[:, 0:C], FF[:, j, :], AW[:, AW_W2 + C * j:AW_W2 + C * (j + 1)],
                                          start=(j == 0), stop=(j == FT - 1))
                mm.then_inc(ff_mm, 1)
                return 4 * FT * P

            def turn_input(m):
                pe.wait_ge(ln3_done, m + 1)
                nc.tensor.transpose(b_t[0:C, 0:P], LN3[:], ident).then_inc(xt_mm, 1)
                return 2 * P

            def turn_states(m):
                pe.wait_ge(hf_done, 2 * (m + 1))
                pe.wait_ge(xt_done, min(m + 2, NT))
                nc.tensor.transpose(b_t[:, 0:C], HF[:].rearrange("p b s -> p (b s)"), ident[0:C, 0:C]).then_inc(out_mm, 1)
                return 2 * P

            def beside(g):
                cols = 0
                for m, o in at(g):
                    if o == FIRST:
                        cols += queries(m)
                    if m == 0 and o in (FIRST, FIRST + 1, 0, 1):
                        values((FIRST, FIRST + 1, 0, 1).index(o))
                    ahead = 2 if m == 0 else 0
                    if o + ahead in range(0, 2 * NU, 2):
                        cols += scores(m, (o + ahead) // 2)
                    if o in range(3, 3 + 2 * NU, 2):
                        cols += turn_probs(m, (o - 3) // 2)
                    if o in range(5, 5 + 2 * NU, 2):
                        cols += weigh(m, (o - 5) // 2)
                    if o == 22:
                        cols += project(m)
                    if o == 24:
                        cols += widen(m)
                    if o == 27:
                        cols += narrow(m)
                    if o == 34:
                        cols += turn_input(m)
                if leaving(g) is not None:
                    cols += turn_states(leaving(g))
                return cols

            def preload(s, gate, dst, width, off, first):
                m, c = divmod(s // CHUNK, STEPS // CHUNK)
                o = dst[0:C, 0:CHUNK * width].rearrange("p (s q) -> p s q", q=width)[:, :, off:off + B]
                r = XT[:, m, :, CHUNK * c:CHUNK * (c + 1)].rearrange("p b s -> p s b")
                nc.tensor.matmul(o, UW[:, gate, :], r, start=first, stop=True, skip_group_check=True)

            def preload_ig(s):
                if s >= 1:
                    pe.wait_ge(gates, s)
                pe.wait_ge(xt_done, s // STEPS + 1)
                preload(s, 0, b_ig, 2 * B, 0, True)
                preload(s, 1, b_ig, 2 * B, B, False)

            for g in EVERY:
                if g == 0:
                    pe.wait_ge(lw_done, 6)
                    pe.wait_ge(zeroed, 10)
                    preload_ig(0)
                if 0 <= g < LAST:
                    sc = g % CHUNK
                    if g >= 1:
                        pe.wait_ge(h_done, g)
                    for gate in range(2):
                        for r in (slice(0, HC), slice(HC, C)):
                            mm = nc.tensor.matmul(b_ig[r, 8 * sc + 4 * gate:8 * sc + 4 * gate + 4], VW[:, gate, r],
                                                  H[:, g % STEPS, :], start=False, stop=True, skip_group_check=True)
                    mm.then_inc(ig_mm, 1)
                    if sc == 0:
                        preload(g, 2, b_o, B, 0, True)
                    nc.tensor.matmul(b_o[0:C, 4 * sc:4 * sc + 4], VW[:, 2, :], H[:, g % STEPS, :], start=False,
                                     stop=True, skip_group_check=True).then_inc(o_mm, 1)
                cols = beside(g)
                if any(o in (0, 23) for _, o in at(g)):
                    cols -= COLS_TABLE
                if 0 <= g < LAST:
                    if (g + 1) % CHUNK == 0 and g + 1 < LAST:
                        fill(COLS_STEP // 3 - cols, b_fill)
                        preload_ig(g + 1)
                    else:
                        fill(COLS_STEP - cols, b_fill)
                elif start(0) + 5 <= g < 0:
                    fill(COLS_EARLY - cols, b_fill)

        @block.scalar
        def _(act):
            act.dma_start(K[:], consts).then_inc(ld_k, 16)
            act.dma_start(X[:], x_fm).then_inc(ld_x1, 16)
            act.dma_start(LW[:], lstm_w).then_inc(ld_lw, 16)

            act.wait_ge(gn_rs, 1)
            act.wait_ge(xn_done, 2)
            for j in range(2):
                nc.scalar.copy(XC[:, j, :].rearrange("p (y x) -> p y x", y=SIDE), XN[:, j, 1:SIDE + 1, 1:SIDE + 1]
                               ).then_inc(xc_done, 1)

            def z_out(i):
                b, pt = divmod(i, 2)
                for m in range(2):
                    act.wait_ge(z_mm, 2 * i + m + 1)
                    nc.scalar.copy(Z[:, pt, b, :, :].rearrange("p k f -> p (k f)")[:, 288 * m:288 * (m + 1)],
                                   b_z[2 * (i % 3) + m][:, 0:288]).then_inc(z_sb, 1)

            act.wait_ge(om_mm, 1)
            for j in range(2):
                nc.scalar.activation(OM[:, j, :], b_om[0:2 * OFFS, N * j:N * (j + 1)], ACT.Identity, bias=OB
                                     ).then_inc(om_low, 1)
            z_out(0)
            act.wait_ge(omt_done, 1)
            for i in range(4):
                j, h = divmod(i, 2)
                src = b_omt[:, 54 * i:54 * (i + 1)].rearrange("p (b o) -> p b o", b=2)[:, :, 18:27]
                nc.scalar.activation(MK[:, 2 * j:2 * j + 2, :, h], src, ACT.Tanh, scale=0.5).then_inc(mask_act, 1)
            def hats_abs(b):
                v = HAT[:, :, b, :, :, :].rearrange("p d k h v -> p d (k h v)")
                act.wait_ge(dist, b + 1)
                nc.scalar.activation(v, v, ACT.Abs).then_inc(hat_abs, 1)

            def hats_relu(b):
                v = HAT[:, :, b, :, :, :].rearrange("p d k h v -> p d (k h v)")
                act.wait_ge(hat_abs, b + 1)
                nc.scalar.activation(v, v, ACT.Relu, bias=1.0, scale=-1.0).then_inc(hat_act, 1)

            z_out(1)
            z_out(2)
            hats_abs(0)
            hats_relu(0)
            for i in range(3, 2 * B):
                z_out(i)
            for g, (b, k) in enumerate(GROUPS):
                if k == HATS_AT and b + 1 < B:
                    hats_abs(b + 1)
                if k == HATS_AT + 2 and b + 1 < B:
                    hats_relu(b + 1)
                act.wait_ge(at_mm, g + 1)
                if g >= 4:
                    act.wait_ge(cv_mm, g - 3)
                nc.scalar.copy(AT[:, g % 4, :, :, :].rearrange("p a h q -> p (a h q)"), b_at[g % 3][:]
                               ).then_inc(at_sb, 1)
            act.wait_ge(zeroed, 10)
            act.wait_ge(t0_mm, 2)
            nc.scalar.copy(T0[:, 4:8, :].rearrange("p n c -> p (n c)"), b_t0[1][:, 0:4 * C]).then_inc(t0_sb, 1)
            act.wait_ge(ln0_st, 1)
            nc.scalar.copy(T0[:, 0:4, :].rearrange("p n c -> p (n c)"), b_t0[0][:, 0:4 * C]).then_inc(t0_sb, 1)
            for i in range(2):
                act.wait_ge(yt_mm, i + 1)
                nc.scalar.copy(YF[0:C, :, P * i:P * (i + 1)].rearrange("p b (n t) -> p n b t", n=4),
                               banks[1 + i][0:C, :].rearrange("p (n b t) -> p n b t", n=4, b=B)).then_inc(yf_done, 1)
            for i in range(4):
                hg, m = divmod(i, 2)
                act.wait_ge(k_mm, i + 1)
                nc.scalar.copy(KF[:, hg, 2 * m:2 * m + 2, :].rearrange("p b q -> p (b q)"), banks[3 + i][:]
                               ).then_inc(k_sb, 1)

            def blocks(m, hg, heads):
                act.wait_ge(q_mm, m + 1)
                if m >= 1:
                    act.wait_ge(s_mm, NU * m)
                for h in heads:
                    r = slice(HD * h, HD * (h + 1))
                    nc.scalar.mul(QB[r, hg, :, h, :], b_et[r, P * hg:P * (hg + 1)].rearrange("p (b t) -> p b t", b=B),
                                  HD ** -0.5).then_inc(q_done, 1)

            def exponents(m, u):
                i = NU * m + u
                act.wait_ge(s_max, i + 1)
                if i >= 2:
                    act.wait_ge(et_mm, i - 1)
                nc.scalar.activation(E[:, i % 2, :], b_s[i % 2][:, 0:N], ACT.Exp, bias=nmax[:, i % 2:i % 2 + 1],
                                     accum_out=rsum[:, i % 2:i % 2 + 1]).then_inc(e_done, 1)

            def turned(m, u):
                i = NU * m + u
                act.wait_ge(et_mm, i + 1)
                if i >= 2:
                    act.wait_ge(pv_mm, i - 1)
                nc.scalar.copy(ET[:, i % 2, :, :].rearrange("p h q -> p (h q)"), b_et[:, 0:N]).then_inc(et_sb, 1)

            def table_for(function):
                nc.scalar.activation(scrap[:], half_neg[0:1, 0:1], function)

            def gelu(m):
                act.wait_ge(h_mm, m + 1)
                nc.scalar.activation(GE[:].rearrange("p j q -> p (j q)"), b_t[:, 0:FT * P], ACT.Gelu).then_inc(ge_done, 1)

            act.wait_ge(zeroed, 10)
            for g in EVERY:
                if 0 <= g < LAST:
                    sc = g % CHUNK
                    act.wait_ge(ig_mm, g + 1)
                    nc.scalar.activation(SA[:, :, :, 2], b_ig[0:C, 8 * sc:8 * sc + 8].rearrange("p (g b) -> p g b", g=2),
                                         ACT.Tanh).then_inc(gates, 1)
                    act.wait_ge(o_mm, g + 1)
                    nc.scalar.activation(TO[:], b_o[0:C, 4 * sc:4 * sc + 4], ACT.Tanh).then_inc(o_gate, 1)
                    act.wait_ge(cell, g + 1)
                    nc.scalar.activation(TC, CS[:, :, 3], ACT.Tanh, scale=0.5).then_inc(tanh_c, 1)
                for m, o in at(g):
                    if o in range(-4, 0):
                        hg, part = divmod(o + 4, 2)
                        blocks(m, hg, range(2 * part, 2 * part + 2))
                    if o == 0:
                        table_for(ACT.Exp)
                    if o in range(1, 1 + 2 * NU, 2):
                        exponents(m, (o - 1) // 2)
                    if o in range(4, 4 + 2 * NU, 2):
                        turned(m, (o - 4) // 2)
                    if o == 23:
                        table_for(ACT.Gelu)
                    if o == 25:
                        gelu(m)

        @block.vector
        def _(dve):
            def link(ins, n=[0]):
                n[0] += 1
                ins.then_inc(v_link, 1)
                dve.wait_ge(v_link, n[0])

            nc.vector.memset(FB[:], 0.0).then_inc(fb_zero, 1)
            dve.wait_ge(ld_x, 16)
            for j in range(2):
                ins = nc.vector.bn_stats(gstat[:, j, :], X2[:, j, :])
            link(ins)
            for j in range(2):
                ins = nc.vector.bn_aggr(gmv[:, j, :], gstat[:, j, :])
            link(ins)
            nc.vector.tensor_copy(gme[:, :, 0:1], gmv[:, :, 0:1]).then_inc(gn_sent, 1)
            link(nc.vector.tensor_tensor(gsq[:], gmv[:, :, 0:1], gmv[:, :, 0:1], ALU.mult))
            nc.vector.tensor_tensor(gme[:, :, 1:2], gsq[:], gmv[:, :, 1:2], ALU.add).then_inc(gn_sent, 1)
            dve.wait_ge(gn_avg, 1)
            link(nc.vector.tensor_copy(gmv[:].rearrange("p j s -> p (j s)"), b_misc[:, 0:4]))
            link(nc.vector.tensor_tensor(gsq[:], gmv[:, :, 0:1], gmv[:, :, 0:1], ALU.mult))
            nc.vector.tensor_tensor(gvar[:], gmv[:, :, 1:2], gsq[:], ALU.subtract).then_inc(gn_var, 1)
            dve.wait_ge(zeroed, 10)
            dve.wait_ge(gn_rs, 1)
            for j in range(2):
                nc.vector.tensor_scalar(XN[:, j, 1:SIDE + 1, 1:SIDE + 1],
                                        X2[:, j, :].rearrange("p (y x) -> p y x", y=SIDE),
                                        gmv[:, j, 0:1], grs[:, j, :], ALU.subtract, ALU.mult).then_inc(xn_done, 1)
            for j in range(2):
                dve.wait_ge(om_low, j + 1)
                nc.vector.tensor_tensor(OM[:, j, :], b_om[C:C + 2 * OFFS, N * j:N * (j + 1)], OM[:, j, :], ALU.add
                                        ).then_inc(om_sb, 1)
            dve.wait_ge(ld_k, 16)
            dve.wait_ge(omt_done, 1)
            dve.wait_ge(mask_act, 4)
            for i in range(4):
                j, h = divmod(i, 2)
                src = b_omt[:, 54 * i:54 * (i + 1)].rearrange("p (b o) -> p b o", b=2)[:, :, 0:18].rearrange(
                    "p b (k d) -> p b k d", d=2)
                for bb in range(2):
                    ins = nc.vector.tensor_tensor(POS[:, :, 2 * j + bb, :, h].rearrange("p d k -> p k d"),
                                                  src[:, bb], base[:, h], ALU.add)
            link(ins)
            pos = POS[:].rearrange("p d b k h -> p (d b k h)")
            nc.vector.tensor_scalar(MK[:], MK[:], 0.5, 0.5, ALU.mult, ALU.add)
            link(nc.vector.tensor_scalar(pos, pos, 0.0, float(SIDE + 1), ALU.max, ALU.min))
            def distances(b):
                kh = TAPS * HALVES
                p_b = POS[:, :, b, :, :].rearrange("p d k h -> p d (k h)")
                nc.vector.tensor_tensor(HAT[:, :, b, :, :, :].rearrange("p d k h v -> p d (k h) v"),
                                        p_b[:, :, :, None].to_broadcast([P, 2, kh, SIDE]),
                                        grid[:, None, None, :].to_broadcast([P, 2, kh, SIDE]),
                                        ALU.subtract).then_inc(dist, 1)

            def masked(b):
                dve.wait_ge(hat_act, b + 1)
                v = HAT[:, 0, b, :, :, :].rearrange("p k h v -> p (k h) v")
                m = MK[:, b, :, :].rearrange("p k h -> p (k h)")
                link(nc.vector.tensor_tensor(v, v, m[:, :, None].to_broadcast([P, TAPS * HALVES, SIDE]), ALU.mult))

            def sampled(b):
                dve.wait_ge(cv_mm, TAPS * (b + 1))
                if b == 0:
                    dve.wait_ge(ld_x1, 16)
                low, high = (b_cv[b % 2][C * i:C * (i + 1), 0:N].rearrange("p (n t) -> p n t", t=TT) for i in range(2))
                nc.vector.tensor_tensor(T0F[:, :, b, :], low, X[:, b, :].rearrange("p (n t) -> p n t", t=TT), ALU.add
                                        ).then_inc(t0f_done, 1)
                dve.wait_ge(t0f_done, 2 * b + 1)
                nc.vector.tensor_tensor(T0F[:, :, b, :], high, T0F[:, :, b, :], ALU.add).then_inc(t0f_done, 1)

            distances(0)
            distances(1)
            for g, (b, k) in enumerate(GROUPS):
                if k == 0:
                    masked(b)
                if k == 3 and b + 2 < B:
                    distances(b + 2)
                if g >= 4:
                    dve.wait_ge(at_mm, g - 3)
                sh = [P, HALVES, SIDE, SIDE]
                nc.vector.tensor_tensor(A[:, g % 4, :, :].rearrange("p h (y x) -> p h y x", y=SIDE),
                                        HAT[:, 0, b, k, :, :, None].to_broadcast(sh),
                                        HAT[:, 1, b, k, :, None, :].to_broadcast(sh), ALU.mult).then_inc(a_done, 1)
                if k == 7 and b >= 1:
                    sampled(b - 1)
            sampled(B - 1)

            for i in range(2):
                if i == 0:
                    dve.wait_ge(t0_mm, 1)
                else:
                    dve.wait_ge(t0_sb, 1)
                for n in range(4 * i, 4 * i + 4):
                    tokens = b_t0[0][:, C * n:C * (n + 1)] if i == 0 else T0[:, n, :]
                    ins = nc.vector.bn_stats(st0[:, n, :], tokens)
                ins.then_inc(ln0_st, 1)
                dve.wait_ge(ln0_st, i + 1)
                for n in range(4 * i, 4 * i + 4):
                    nc.vector.bn_aggr(mv0[:, n, :], st0[:, n, :]).then_inc(ln0_mv, 1)
            dve.wait_ge(t0_sb, 2)
            for n in range(NT):
                if n % 4 == 0:
                    dve.wait_ge(ln0_rs, n // 4 + 1)
                nc.vector.tensor_scalar(Y[:, n, :], T0[:, n, :], mv0[:, n, 0:1], rs0[:, n, :], ALU.subtract,
                                        ALU.mult).then_inc(y_done, 1)
            dve.wait_ge(yb_done, 2)

            def values_out(b):
                dve.wait_ge(v_mm, b + 1)
                nc.vector.tensor_copy(V[:, b, :, :].rearrange("p h d -> p (h d)"), b_v[b][:]).then_inc(v_sb, 1)

            def largest(m, u):
                i = NU * m + u
                dve.wait_ge(s_mm, i + 1)
                nc.vector.tensor_reduce(nmax[:, i % 2:i % 2 + 1], b_s[i % 2][:, 0:N], AX.X, ALU.max, negate=True
                                        ).then_inc(s_max, 1)

            def inverse_sum(m, u):
                i = NU * m + u
                dve.wait_ge(e_done, i + 1)
                nc.vector.reciprocal(rinv[:, i % 2:i % 2 + 1], rsum[:, i % 2:i % 2 + 1]).then_inc(e_inv, 1)

            def normalised(m, u):
                i = NU * m + u
                dve.wait_ge(e_inv, i + 1)
                nc.vector.tensor_scalar(E[:, i % 2, :], E[:, i % 2, :], rinv[:, i % 2:i % 2 + 1], None, ALU.mult
                                        ).then_inc(e_norm, 1)

            def head_out(m, hg, h):
                dve.wait_ge(pv_mm, NU * m + B * (hg + 1))
                r = slice(HD * h, HD * (h + 1))
                nc.vector.tensor_copy(O[r, hg, :, :], b_w[hg][r, :].rearrange("p (b h t) -> p b h t", b=B, h=HPG)[:, :, h, :]
                                      ).then_inc(o_done, 1)

            def norm_stats(m, j, src):
                nc.vector.bn_stats(st[:, j, :], src).then_inc(st_done, 1)

            def norm_aggr(m, j):
                dve.wait_ge(st_done, 3 * m + j + 1)
                nc.vector.bn_aggr(mv[:, j, :], st[:, j, :]).then_inc(t_mv, 1)

            def norm_apply(m, j, dst, src):
                dve.wait_ge(t_rs, 3 * m + j + 1)
                return nc.vector.tensor_scalar(dst, src, mv[:, j, 0:1], rs[:, j, :], ALU.subtract, ALU.mult)

            def first(g):
                for m, o in at(g):
                    if m == 0 and o in (FIRST, FIRST + 1, 3, 4):
                        values_out((FIRST, FIRST + 1, 3, 4).index(o))
                    if m == 0 and o == 6:
                        dve.wait_ge(v_sb, B)
                        nc.vector.memset(CS, 0.0).then_inc(cs_zero, 1)
                    if m == 0 and o in range(0, 2 * NU, 2):
                        largest(m, o // 2)
                    if m > 0 and o in range(1, 1 + 2 * NU, 2):
                        largest(m, (o - 1) // 2)
                    if o in range(2, 2 + 2 * NU, 2):
                        inverse_sum(m, (o - 2) // 2)
                    if o == 23:
                        dve.wait_ge(y_mm, m + 1)
                        nc.vector.tensor_scalar(AY[0:C, :], b_t[0:C, P:2 * P], AW[0:C, AW_BO:AW_BO + 1], None, ALU.add
                                                ).then_inc(ay_done, 1)
                    if o == 25:
                        norm_apply(m, 0, X1[:], R1[:]).then_inc(t_link, 1)
                    if o == 28:
                        dve.wait_ge(ff_mm, m + 1)
                        dve.wait_ge(t_link, 5 * m + 3)
                        nc.vector.tensor_tensor(R2[:], b_t[:, 0:C], X1[:], ALU.add).then_inc(r_done, 1)
                    if o == 30:
                        norm_apply(m, 1, R2[:], R2[:]).then_inc(t_link, 1)
                    if o == 31:
                        dve.wait_ge(t_link, 5 * m + 5)
                        nc.vector.tensor_tensor(T1[:, m, :], R2[:], TB[:, m, :], ALU.add).then_inc(t1_done, 1)
                    if o == 33:
                        norm_apply(m, 2, LN3[:], T1[:, m, :]).then_inc(ln3_done, 1)
                    if o == 36:
                        dve.wait_ge(xt_mm, m + 1)
                        nc.vector.tensor_copy(XT[0:C, m, :, :].rearrange("p b t -> p (b t)"), b_t[0:C, 0:P]
                                              ).then_inc(xt_done, 1)
                if g == LAST:
                    dve.wait_ge(h_done, LAST)
                    dve.wait_ge(out_mm, NT - 1)
                    nc.vector.tensor_copy(HF[:, :, 0:STEPS - 1], H[0:C, 1:STEPS, :].rearrange("p s b -> p b s")
                                          ).then_inc(hf_done, 1)
                    nc.vector.tensor_copy(HF[:, :, STEPS - 1], H[0:C, 0, :]).then_inc(hf_done, 1)
                if leaving(g - 1) is not None:
                    m = leaving(g - 1)
                    dve.wait_ge(out_mm, m + 1)
                    if m >= 2:
                        dve.wait_ge(stored, 16 * (m - 1))
                    nc.vector.scalar_tensor_tensor(out=OUT[:, m % 2, :], in0=b_t[:, 0:C], scalar=0.5, in1=T1[:, m, :],
                                                   op0=ALU.mult, op1=ALU.add).then_inc(out_add, 1)

            def second(g):
                for m, o in at(g):
                    if o in range(2, 2 + 2 * NU, 2):
                        normalised(m, (o - 2) // 2)
                    if o == 20:
                        head_out(m, 1, 0)
                        head_out(m, 1, 1)
                    if o == 21:
                        head_out(m, 1, 3)
                    if o == 23:
                        nc.vector.tensor_tensor(R1[:], b_t[:, 0:C], YB[:, m, :], ALU.add).then_inc(r_done, 1)
                    if o == 24:
                        norm_aggr(m, 0)
                    if o == 29:
                        norm_aggr(m, 1)
                    if o == 32:
                        norm_aggr(m, 2)

            def third(g):
                for m, o in at(g):
                    if o == 26:
                        dve.wait_ge(ge_done, m + 1)
                        nc.vector.tensor_tensor(FF[:].rearrange("p j q -> p (j q)"), b_t[:, FT * P:2 * FT * P],
                                                GE[:].rearrange("p j q -> p (j q)"), ALU.mult).then_inc(ff_done, 1)
                    if o in range(12, 12 + HPG):
                        head_out(m, 0, o - 12)
                    if o == 20:
                        head_out(m, 1, 2)
                    if o == 23:
                        dve.wait_ge(r_done, 2 * m + 1)
                        norm_stats(m, 0, R1[:])
                    if o == 25:
                        dve.wait_ge(t_link, 5 * m + 1)
                        nc.vector.tensor_tensor(X1[:], X1[:], VEC[:, VEC_G1, :], ALU.mult).then_inc(t_link, 1)
                    if o == 26:
                        dve.wait_ge(t_link, 5 * m + 2)
                        nc.vector.tensor_tensor(X1[:], X1[:], VEC[:, VEC_B1, :], ALU.add).then_inc(t_link, 1)
                    if o == 28:
                        dve.wait_ge(r_done, 2 * m + 2)
                        norm_stats(m, 1, R2[:])
                    if o == 30:
                        dve.wait_ge(t_link, 5 * m + 4)
                        nc.vector.tensor_tensor(R2[:], R2[:], VEC[:, VEC_G2, :], ALU.mult).then_inc(t_link, 1)
                    if o == 31:
                        dve.wait_ge(t1_done, m + 1)
                        norm_stats(m, 2, T1[:, m, :])

            for g in EVERY:
                cell_step = 0 <= g < LAST
                first(g)
                if cell_step:
                    if g >= 1:
                        dve.wait_ge(h_done, g)
                    else:
                        dve.wait_ge(cs_zero, 1)
                    nc.vector.scalar_tensor_tensor(out=SA[:, 0, :, 3], in0=H[0:C, g % STEPS, :], scalar=0.5,
                                                   in1=CS[:, :, 3], op0=ALU.mult, op1=ALU.mult).then_inc(u_done, 1)
                second(g)
                if cell_step:
                    dve.wait_ge(gates, g + 1)
                    dve.wait_ge(u_done, g + 1)
                    nc.vector.tensor_tensor_scan(CS.rearrange("p b q -> p (b q)"),
                                                 SA[:, 0, :, :].rearrange("p b q -> p (b q)"),
                                                 SA[:, 1, :, :].rearrange("p b q -> p (b q)"), 0.0,
                                                 op0=ALU.add, op1=ALU.mult).then_inc(cell, 1)
                third(g)
                if cell_step:
                    dve.wait_ge(tanh_c, g + 1)
                    dve.wait_ge(o_gate, g + 1)
                    if g % STEPS == 0 and g >= STEPS:
                        dve.wait_ge(hf_done, 2 * (g // STEPS))
                    nc.vector.scalar_tensor_tensor(out=H[0:C, (g + 1) % STEPS, :], in0=TO[:], scalar=1.0, in1=TC,
                                                   op0=ALU.add, op1=ALU.mult).then_inc(h_done, 1)


def shape_constants():
    k = np.zeros((P, K_END), np.float32)
    p = np.arange(P)
    k[p, K_ID + p] = 1.0
    k[:, K_PAIR:K_PAIR + P] = np.where(p[:, None] // 2 == p[None, :] // 2, 0.5, 0.0)
    k[:, K_MASK:K_MASK + HPG] = np.where(p[:, None] // HD == np.arange(HPG)[None, :], HD ** -0.5, 0.0)
    base = np.zeros((P, HALVES, TAPS, 2), np.float32)
    for h in range(HALVES):
        for t in range(TAPS):
            base[:, h, t, 0] = (P * h + p) // SIDE + 1 + t // 3 - 1
            base[:, h, t, 1] = p % SIDE + 1 + t % 3 - 1
    k[:, K_BASE:K_BASE + 36] = base.reshape(P, 36)
    k[:, K_GRID:K_GRID + SIDE] = np.arange(1, SIDE + 1)
    return k


def packed(i):
    f = {n: np.asarray(a) for n, a in i.items()}
    x = f["x"].reshape(B // 2, 2, N, C)
    a = {}
    a["x_fm2"] = np.ascontiguousarray(x.transpose(1, 3, 0, 2).reshape(P, 2, N))
    a["x_fm"] = np.ascontiguousarray(f["x"].reshape(B, N, C).transpose(2, 0, 1))
    cw = np.zeros((P, CW_END), np.float32)
    ow = f["L0_conv_offset_w"].reshape(TAPS, C, OFFS).transpose(1, 0, 2)
    dcn = np.zeros((P, 2, TAPS * C), np.float32)
    dw = f["L0_conv_dcn_weight"].transpose(1, 2, 3, 0).reshape(C, TAPS * C)
    for h in range(2):
        r = slice(C * h, C * (h + 1))
        cw[r, 0:CW_OB].reshape(C, TAPS, 2, OFFS)[:, :, h, :] = ow
        dcn[r, h] = dw
        cw[OFFS * h:OFFS * (h + 1), CW_OB] = f["L0_conv_offset_b"].reshape(OFFS)
    a["conv_w"] = cw
    a["dcn_w"] = dcn
    aw = np.zeros((P, AW_END), np.float32)
    aw[0:C, AW_QKV:AW_OUT] = f["L1_attn_w_qkv"].T
    aw[:, AW_OUT:AW_W1] = f["L1_attn_w_out"].T.reshape(HG, P, C).transpose(1, 0, 2).reshape(P, HG * C)
    aw[0:C, AW_W1:AW_WV] = f["L1_attn_w1"].T
    aw[0:C, AW_WV:AW_W2] = f["L1_attn_wv"].T
    aw[:, AW_W2:AW_BO] = f["L1_attn_w2"].T.reshape(FT, P, C).transpose(1, 0, 2).reshape(P, FT * C)
    aw[0:C, AW_BO] = f["L1_attn_b_out"]
    a["attn_w"] = aw
    lw = np.zeros((C + 1, LW_END), np.float32)
    for j, g in enumerate("ico"):
        lw[0:C, LW_V + C * j:LW_V + C * (j + 1)] = f[f"L1_ffn_V_{g}"]
        lw[0:C, LW_U + C * j:LW_U + C * (j + 1)] = f[f"L1_ffn_U_{g}"]
        lw[C, LW_U + C * j:LW_U + C * (j + 1)] = f[f"L1_ffn_b_{g}"]
    a["lstm_w"] = lw
    a["vecs"] = np.stack([f[f"L1_attn_{n}"] for n in ("b_out", "ln1_g", "ln1_b", "ln2_g", "ln2_b")])
    a["consts"] = shape_constants()
    return a


def kernel(**inputs):
    import concourse.bacc as _bacc
    from concourse.bass_utils import run_bass_kernel_spmd as _run

    nc = _bacc.Bacc("TRN2", target_bir_lowering=False, num_devices=1)
    arrays = packed(inputs)
    args = [nc.dram_tensor(f"in_{n}", a.shape, F32, kind="ExternalInput").ap() for n, a in arrays.items()]
    out = nc.dram_tensor("out_0_dram", (NT, P, C), F32, kind="ExternalOutput").ap()
    hybrid_kernel(nc, *args, out)
    r = _run(nc, [{f"in_{n}": a for n, a in arrays.items()}], core_ids=[0])
    tiles = r.results[0]["out_0_dram"].reshape(NT, B, TT, C)
    return tiles.transpose(1, 0, 2, 3).reshape(B, SIDE, SIDE, C)
```

```python
from contextlib import ExitStack

import numpy as np

import concourse.bass as bass
from concourse import mybir

F32 = mybir.dt.float32
BF16 = mybir.dt.bfloat16
ALU = mybir.AluOpType
ACT = mybir.ActivationFunctionType
AX = mybir.AxisListType

P = 128
B, SIDE, C = 4, 16, 64
N = SIDE * SIDE
TAPS = 9
OFFS = 3 * TAPS
OFFS2 = 2 * OFFS
ZC = TAPS * C // 2
HALVES = N // P
HEADS, HD = 8, 32
HG = HEADS * HD // P
HPG = HEADS // HG
DFF = 256
FT = DFF // P
TT = 32
NT = N // TT
STEPS = TT
HC = C // 2
CHUNK = 16
HATS_AT = 3
FIRST = QUERIES = -5
BLOCKS = -4
EXP_TABLE = 0
HEADS_0 = 13
HEADS_1 = 20
PROJECT = 21
PROJECTED = GELU_TABLE = 22
WIDEN, GELU, GATED = 23, 24, 25
NARROW, NARROWED = 26, 27
NORM_1, NORM_2 = 24, 29
TOKENS = 30
AGGR = (23, 28, 31)
CELL_INPUT = 32
CELL_READY = 33
LEAD = 34
OUT_LAG = 2
GN_EPS = LN_EPS = 1e-5
COLS_LOAD = 4608
COLS_GROUPS = 4096
COLS_LN = 5632
COLS_TURN = 256
COLS_TURNED = 2048
COLS_EARLY = 1000
COLS_STEP = 2000
COLS_TABLE = 1500

K_ID, K_PAIR = 0, P
K_BASE = K_PAIR + P
K_GRID = K_BASE + HALVES * TAPS * 2
K_END = K_GRID + SIDE
CW_OW, CW_OB = 0, TAPS * OFFS2
CW_END = CW_OB + 1
AW_QKV, AW_OUT, AW_W1, AW_WV = 0, 768, 768 + HG * C, 768 + HG * C + DFF
AW_W2 = AW_WV + DFF
AW_BO = AW_W2 + FT * C
AW_END = AW_BO + 1
LW_V, LW_U, LW_END = 0, 3 * C, 6 * C
VEC_BO, VEC_G1, VEC_B1, VEC_G2, VEC_B2 = range(5)


def hybrid_kernel(nc, x_fm2, x_fm, conv_w, dcn_w, attn_w, lstm_w, vecs, consts, out):
    ctx = ExitStack()
    with ctx:
        def sb(name, shape, dt=F32):
            return ctx.enter_context(nc.sbuf_tensor(name, shape, dt))

        def bank(name):
            return ctx.enter_context(nc.psum_tensor(name, [P, 512], F32))

        def sem(name):
            return ctx.enter_context(nc.semaphore(name))

        X2 = sb("X2", [P, 2, N])
        X = sb("X", [C, B, N])
        CW = sb("CW", [P, CW_END])
        DW = sb("DW", [P, 2, TAPS * C])
        AW = sb("AW", [P, AW_END])
        LW = sb("LW", [C + 1, LW_END])
        VEC = sb("VEC", [P, 5, C])
        K = sb("K", [P, K_END])
        ident = K[:, K_ID:K_ID + P]
        pair = K[:, K_PAIR:K_PAIR + P]
        base = K[:, K_BASE:K_GRID].rearrange("p (h k d) -> p h k d", h=2, d=2)
        grid = K[:, K_GRID:K_GRID + SIDE]
        OW = CW[:, CW_OW:CW_OB].rearrange("p (t o) -> p t o", t=TAPS)
        OB = CW[0:OFFS2, CW_OB:CW_OB + 1]

        gstat = sb("gstat", [P, 2, 6])
        gmv = sb("gmv", [P, 2, 2])
        gsq = sb("gsq", [P, 2, 1])
        gme = sb("gme", [P, 2, 2])
        gvar = sb("gvar", [P, 2, 1])
        grs = sb("grs", [P, 2, 1])
        XN = sb("XN", [P, 2, SIDE + 2, SIDE + 2])
        XC = sb("XC", [P, 2, N])
        OM = sb("OM", [OFFS2, 2, N])
        POS = sb("POS", [P, 2, B, TAPS, HALVES])
        MK = sb("MK", [P, B, TAPS, HALVES])
        HAT = sb("HAT", [P, 2, B, TAPS, HALVES, SIDE])
        A = sb("A", [P, 4, HALVES, N])
        AT = sb("AT", [P, 4, 2, HALVES, P])
        Z = sb("Z", [P, 2, B, TAPS, C])
        T0F = sb("T0F", [C, NT, B, TT])
        T0 = sb("T0", [P, NT, C])
        st0 = sb("st0", [P, NT, 6])
        mv0 = sb("mv0", [P, NT, 2])
        rs0 = sb("rs0", [P, NT, 1])
        Y = sb("Y", [P, NT, C])
        YB = sb("YB", [P, NT, C])
        TB = sb("TB", [P, NT, C])
        YF = sb("YF", [P, B, N])
        KF = sb("KF", [P, HG, B, N])
        V = sb("V", [P, B, HALVES, HEADS * HD])
        QB = sb("QB", [P, HG, B, HPG, TT])
        nmax = sb("nmax", [P, 2])
        rsum = sb("rsum", [P, 2])
        rinv = sb("rinv", [P, 2])
        E = sb("E", [P, 2, N])
        ET = sb("ET", [P, 2, HALVES, P])
        O = sb("O", [P, HG, B, TT])
        AY = sb("AY", [P, P])
        R1 = sb("R1", [P, C])
        R2 = sb("R2", [P, C])
        X1 = sb("X1", [P, C])
        GE = sb("GE", [P, FT, P])
        FF = sb("FF", [P, FT, P])
        st = sb("st", [P, 3, 6])
        mv = sb("mv", [P, 3, 2])
        rs = sb("rs", [P, 3, 1])
        half_neg = sb("half_neg", [P, NT])
        T1 = sb("T1", [P, NT, C])
        LN3 = sb("LN3", [P, C])
        XT = sb("XT", [C + 1, NT, B, TT])
        VW = sb("VW", [P, 3, C])
        UW = sb("UW", [C + 1, 3, C])
        H = sb("H", [P, STEPS, B])
        HF = sb("HF", [C, B, TT])
        SA = sb("SA", [C, 2, B, 3])
        TO = sb("TO", [C, B])
        OUT = sb("OUT", [P, 2, C])
        scrap = sb("scrap", [1, 1])
        FB = sb("FB", [P, 512], BF16)

        banks = [bank(f"bank{i}") for i in range(8)]
        b_misc, b_om, b_omt = banks[0], banks[1], banks[2]
        b_z = banks[3:8] + banks[0:1]
        b_at = banks[1:4]
        b_cv = banks[4:6]
        b_t0 = (banks[0], banks[6])
        b_ig, b_o, b_fill, b_s0, b_s1, b_et, b_pv, b_t = banks
        b_s = [b_s0, b_s1]
        b_v = [b_t, b_ig, b_o, b_pv]
        b_w = [b_pv, b_t]
        CS = b_o[C:P, 0:3 * B].rearrange("p (b q) -> p b q", q=3)
        TC = b_o[C:P, 3 * B:4 * B]

        ld_x, ld_x1, ld_cw, ld_dw, ld_aw, ld_lw, ld_k, ld_v, zeroed, fb_zero, cs_zero = (sem(n) for n in (
            "ld_x", "ld_x1", "ld_cw", "ld_dw", "ld_aw", "ld_lw", "ld_k", "ld_v", "zeroed", "fb_zero", "cs_zero"))
        v_link = sem("v_link")
        p_link = sem("p_link")
        gn_sent, gn_avg, gn_var, gn_rs, xn_done, xc_done = (sem(n) for n in (
            "gn_sent", "gn_avg", "gn_var", "gn_rs", "xn_done", "xc_done"))
        om_mm, om_low, om_sb, omt_done, mask_act, dist, hat_abs, hat_act = (sem(n) for n in (
            "om_mm", "om_low", "om_sb", "omt_done", "mask_act", "dist", "hat_abs", "hat_act"))
        z_mm, z_sb, a_done, at_mm, at_sb, cv_mm, t0f_done = (sem(n) for n in (
            "z_mm", "z_sb", "a_done", "at_mm", "at_sb", "cv_mm", "t0f_done"))
        t0_mm, t0_sb, ln0_st, ln0_mv, ln0_rs, y_done, yt_mm, yf_done = (sem(n) for n in (
            "t0_mm", "t0_sb", "ln0_st", "ln0_mv", "ln0_rs", "y_done", "yt_mm", "yf_done"))
        k_mm, k_sb, v_mm, v_sb, yb_done = (sem(n) for n in ("k_mm", "k_sb", "v_mm", "v_sb", "yb_done"))
        q_mm, q_done, s_mm, s_max, e_done, e_inv, e_norm, et_mm, et_sb, pv_mm, o_done, o_act = (sem(n) for n in (
            "q_mm", "q_done", "s_mm", "s_max", "e_done", "e_inv", "e_norm", "et_mm", "et_sb", "pv_mm", "o_done", "o_act"))
        yf_mm = sem("yf_mm")
        y_mm, r_done, ay_done, h_mm, ge_done, ff_done, ff_mm, t_mv, t_rs, t1_done, ln3_done, xt_mm, xt_done = (
            sem(n) for n in ("y_mm", "r_done", "ay_done", "h_mm", "ge_done", "ff_done", "ff_mm", "t_mv",
                             "t_rs", "t1_done", "ln3_done", "xt_mm", "xt_done"))
        t_link = sem("t_link")
        st_done = sem("st_done")
        tp_link = sem("tp_link")
        lw_done, ig_mm, o_mm, gates, o_gate, u_done, cell, tanh_c, h_done = (sem(n) for n in (
            "lw_done", "ig_mm", "o_mm", "gates", "o_gate", "u_done", "cell", "tanh_c", "h_done"))
        hf_done, out_mm, out_add, stored = (sem(n) for n in ("hf_done", "out_mm", "out_add", "stored"))
        block = ctx.enter_context(nc.Block())

        GROUPS = [(b, k) for b in range(B) for k in range(TAPS)]
        UNITS = [(hg, b) for hg in range(HG) for b in range(B)]
        NU = len(UNITS)
        VHEADS = 6
        LAST = NT * STEPS

        def start(m):
            return m * STEPS - LEAD

        def at(g):
            return [(m, g - start(m)) for m in range(NT) if FIRST <= g - start(m) < LEAD]

        def leaving(g):
            m, o = divmod(g - OUT_LAG, STEPS)
            return m - 1 if o == 0 and 1 <= m <= NT else None

        VALUES_AT = (QUERIES, QUERIES + 1, 0, 1)
        VALUES_OUT_AT = (QUERIES, QUERIES + 1, 2, 3)

        EVERY = range(start(0) + FIRST, LAST + OUT_LAG + 2)

        @block.sync
        def _(sp):
            sp.dma_start(X2[:], x_fm2).then_inc(ld_x, 16)
            sp.dma_start(CW[:], conv_w).then_inc(ld_cw, 16)
            sp.dma_start(DW[:], dcn_w).then_inc(ld_dw, 16)
            sp.dma_start(AW[:], attn_w).then_inc(ld_aw, 16)
            sp.dma_start(VEC[:], vecs.rearrange("(o v) c -> o v c", o=1).to_broadcast([P, 5, C])).then_inc(ld_v, 16)
            for m in range(NT):
                sp.wait_ge(out_add, m + 1)
                if m >= 1:
                    sp.wait_ge(stored, 16 * m)
                sp.dma_start(out[m], OUT[:, m % 2, :]).then_inc(stored, 16)
            sp.wait_ge(stored, NT * 16)

        @block.gpsimd
        def _(pool):
            def link(ins, n=[0]):
                n[0] += 1
                ins.then_inc(p_link, 1)
                pool.wait_ge(p_link, n[0])

            nc.gpsimd.memset(XN[:], 0.0).then_inc(zeroed, 1)
            nc.gpsimd.memset(half_neg[:], -0.5).then_inc(zeroed, 1)
            nc.gpsimd.memset(H[:], 0.0).then_inc(zeroed, 1)
            nc.gpsimd.memset(VW[:], 0.0).then_inc(zeroed, 1)
            nc.gpsimd.memset(XT[:], 1.0).then_inc(zeroed, 1)
            nc.gpsimd.memset(SA[:], 1.0).then_inc(zeroed, 1)
            nc.gpsimd.memset(YF[:], 0.0).then_inc(zeroed, 1)
            nc.gpsimd.memset(AY[:], 0.0).then_inc(zeroed, 1)
            nc.gpsimd.memset(QB[:], 0.0).then_inc(zeroed, 1)
            pool.wait_ge(zeroed, 9)
            nc.gpsimd.memset(SA[:, 0, :, 0], 0.0).then_inc(zeroed, 1)
            pool.wait_ge(gn_var, 1)
            link(nc.gpsimd.tensor_scalar(gvar[:], gvar[:], GN_EPS, None, ALU.add))
            nc.gpsimd.tensor_tensor(grs[:, :, 0], gvar[:, :, 0], half_neg[:, 0:2], ALU.pow).then_inc(gn_rs, 1)
            pool.wait_ge(ld_lw, 16)
            for g, s in ((0, 0.5), (1, 1.0), (2, 0.5)):
                nc.gpsimd.tensor_scalar(VW[0:C, g, :], LW[0:C, LW_V + C * g:LW_V + C * (g + 1)], 0.5 * s, None,
                                        ALU.mult).then_inc(lw_done, 1)
                nc.gpsimd.tensor_scalar(UW[:, g, :], LW[:, LW_U + C * g:LW_U + C * (g + 1)], s, None,
                                        ALU.mult).then_inc(lw_done, 1)
            for i in range(2):
                half = slice(4 * i, 4 * i + 4)
                pool.wait_ge(ln0_mv, 4 * (i + 1))
                link(nc.gpsimd.tensor_scalar(rs0[:, half, 0], mv0[:, half, 1], LN_EPS, None, ALU.add))
                nc.gpsimd.tensor_tensor(rs0[:, half, 0], rs0[:, half, 0], half_neg[:, half], ALU.pow).then_inc(ln0_rs, 1)
            pool.wait_ge(ld_v, 16)
            pool.wait_ge(t0_sb, 2)
            nc.gpsimd.tensor_tensor(TB[:], T0[:], VEC[:, VEC_B2:VEC_B2 + 1, :].to_broadcast([P, NT, C]),
                                    ALU.add).then_inc(yb_done, 1)
            pool.wait_ge(y_done, NT)
            nc.gpsimd.tensor_tensor(YB[:], Y[:], VEC[:, VEC_BO:VEC_BO + 1, :].to_broadcast([P, NT, C]),
                                    ALU.add).then_inc(yb_done, 1)
            for g in EVERY:
                for m, o in at(g):
                    if o in AGGR:
                        j = AGGR.index(o)
                        i = 3 * m + j + 1
                        pool.wait_ge(t_mv, i)
                        nc.gpsimd.tensor_scalar(rs[:, j, :], mv[:, j, 1:2], LN_EPS, None, ALU.add).then_inc(tp_link, 1)
                        pool.wait_ge(tp_link, i)
                        nc.gpsimd.tensor_tensor(rs[:, j, :], rs[:, j, :], half_neg[:, 0:1], ALU.pow).then_inc(t_rs, 1)
                if g > 0 and g % STEPS == 0 and g < LAST:
                    m = g // STEPS - 1
                    if m >= 1:
                        pool.wait_ge(out_mm, m)
                    pool.wait_ge(h_done, g)
                    nc.gpsimd.tensor_copy(HF[:, :, 0:STEPS - 1], H[0:C, 1:STEPS, :].rearrange("p s b -> p b s")
                                          ).then_inc(hf_done, 1)
                    nc.gpsimd.tensor_copy(HF[:, :, STEPS - 1], H[0:C, 0, :]).then_inc(hf_done, 1)

        @block.tensor
        def _(pe):
            def fill(cols, idle):
                while cols >= 128:
                    n = min(cols, 512)
                    nc.tensor.matmul(idle[:, 0:n], FB[:, 0:P], FB[:, 0:n], start=True, stop=True)
                    cols -= n

            pe.wait_ge(fb_zero, 1)
            fill(COLS_LOAD, banks[7])
            pe.wait_ge(ld_k, 16)
            pe.wait_ge(gn_sent, 2)
            nc.tensor.matmul(b_misc[:, 0:4], pair, gme[:].rearrange("p j s -> p (j s)"),
                             start=True, stop=True).then_inc(gn_avg, 1)
            fill(COLS_GROUPS, banks[7])
            pe.wait_ge(ld_cw, 16)
            pe.wait_ge(xn_done, 2)
            for t in range(TAPS):
                dy, dx = t // 3, t % 3
                r = slice(C * (t % 2), C * (t % 2) + OFFS2)
                mm = nc.tensor.matmul(b_om[r, :].rearrange("p (j y x) -> p j y x", j=2, y=SIDE), OW[:, t, :],
                                      XN[:, :, dy:dy + SIDE, dx:dx + SIDE], start=(t < 2), stop=(t >= TAPS - 2))
            mm.then_inc(om_mm, 1)

            def z(i):
                b, pt = divmod(i, 2)
                if i >= 3:
                    pe.wait_ge(z_sb, 2 * (i - 2))
                for m in range(2):
                    nc.tensor.matmul(b_z[2 * (i % 3) + m][:, 0:ZC],
                                     XC[:, b // 2, P * pt:P * (pt + 1)], DW[:, b % 2, ZC * m:ZC * (m + 1)],
                                     start=True, stop=True).then_inc(z_mm, 1)

            pe.wait_ge(ld_dw, 16)
            pe.wait_ge(xc_done, 2)
            z(0)
            for i in range(4):
                j, h = divmod(i, 2)
                if h == 0:
                    pe.wait_ge(om_sb, j + 1)
                mm = nc.tensor.transpose(b_omt[:, OFFS2 * i:OFFS2 * (i + 1)], OM[:, j, P * h:P * (h + 1)],
                                         ident[0:OFFS2, 0:OFFS2])
            mm.then_inc(omt_done, 1)
            for i in range(1, 2 * B):
                z(i)

            def turn(g):
                pe.wait_ge(a_done, g + 1)
                if g == 0:
                    pe.wait_ge(dist, 1)
                if g >= 3:
                    pe.wait_ge(at_sb, g - 2)
                for pt in range(2):
                    for h in range(HALVES):
                        q = 2 * pt + h
                        mm = nc.tensor.transpose(b_at[g % 3][:, P * q:P * (q + 1)],
                                                 A[:, g % 4, h, P * pt:P * (pt + 1)], ident)
                mm.then_inc(at_mm, 1)

            def gather(g):
                b, k = GROUPS[g]
                pe.wait_ge(at_sb, g + 1)
                if g == 0:
                    pe.wait_ge(z_sb, 4 * B)
                if k == 0 and b >= 2:
                    pe.wait_ge(t0f_done, 2 * (b - 1))
                for pt in range(2):
                    mm = nc.tensor.matmul(b_cv[b % 2][C * pt:C * (pt + 1), 0:N], Z[:, pt, b, k, :],
                                          AT[:, g % 4, pt, :, :], start=(k == 0), stop=(k == TAPS - 1))
                mm.then_inc(cv_mm, 1)

            for g in range(len(GROUPS) + 1):
                if g < len(GROUPS):
                    turn(g)
                if g >= 1:
                    gather(g - 1)

            pe.wait_ge(t0f_done, 2 * B)
            for n in range(NT):
                mm = nc.tensor.transpose(b_t0[n // 4][:, C * (n % 4):C * (n % 4 + 1)],
                                         T0F[:, n, :, :].rearrange("p b t -> p (b t)"), ident[0:C, 0:C])
                if n % 4 == 3:
                    mm.then_inc(t0_mm, 1)
            fill(COLS_LN, banks[7])
            for i in range(2):
                for n in range(4 * i, 4 * i + 4):
                    pe.wait_ge(y_done, n + 1)
                    mm = nc.tensor.transpose(banks[1 + i][0:C, P * (n % 4):P * (n % 4 + 1)], Y[:, n, :], ident)
                    fill(COLS_TURN, banks[7])
                mm.then_inc(yt_mm, 1)
            fill(COLS_TURNED, banks[7])
            pe.wait_ge(ld_aw, 16)
            pe.wait_ge(zeroed, 10)
            pe.wait_ge(yf_done, 2)
            for i in range(4):
                hg, m = divmod(i, 2)
                nc.tensor.matmul(banks[3 + i][:], AW[:, AW_QKV + 256 + P * hg:AW_QKV + 256 + P * (hg + 1)],
                                 YF[:, 2 * m:2 * m + 2, :], start=True, stop=True).then_inc(k_mm, 1)

            def values(b):
                if b == 3:
                    pe.wait_ge(k_sb, 4)
                for h in range(HALVES):
                    mm = nc.tensor.matmul(b_v[b][:, 256 * h:256 * (h + 1)], YF[:, b, P * h:P * (h + 1)],
                                          AW[:, AW_QKV + 512:AW_QKV + 768], start=True, stop=True)
                mm.then_inc(v_mm, 1)

            def queries(m):
                if m >= 1:
                    pe.wait_ge(et_sb, NU * m)
                else:
                    pe.wait_ge(k_sb, 3)
                for hg in range(HG):
                    mm = nc.tensor.matmul(b_et[:, P * hg:P * (hg + 1)], AW[:, AW_QKV + P * hg:AW_QKV + P * (hg + 1)],
                                          YF[:, :, TT * m:TT * (m + 1)], start=True, stop=True)
                mm.then_inc(q_mm, 1)
                return 4 * HG * P

            def scores(m, u):
                hg, b = UNITS[u]
                i = NU * m + u
                if b == 0:
                    pe.wait_ge(q_done, NU * m + HPG * (hg + 1))
                if i >= 2:
                    pe.wait_ge(e_done, i - 1)
                else:
                    pe.wait_ge(k_sb, 4)
                nc.tensor.matmul(b_s[i % 2][:, 0:N], QB[:, hg, b, :, :].rearrange("p h t -> p (h t)"), KF[:, hg, b, :],
                                 start=True, stop=True).then_inc(s_mm, 1)
                return 4 * N

            def turn_probs(m, u):
                i = NU * m + u
                if u == 0:
                    pe.wait_ge(q_done, NU * (m + 1))
                elif i >= 1:
                    pe.wait_ge(et_sb, i)
                pe.wait_ge(e_norm, i + 1)
                for h in range(HALVES):
                    mm = nc.tensor.transpose(b_et[:, P * h:P * (h + 1)], E[:, i % 2, P * h:P * (h + 1)], ident)
                mm.then_inc(et_mm, 1)
                return 4 * P

            def weigh(m, u):
                hg, b = UNITS[u]
                i = NU * m + u
                pe.wait_ge(et_sb, i + 1)
                if i < B:
                    pe.wait_ge(v_sb, B)
                if u == 0 and m >= 1:
                    pe.wait_ge(ff_done, FT * m)
                if u == B and m >= 1:
                    pe.wait_ge(xt_done, m)
                if u == B and m >= 2:
                    pe.wait_ge(out_add, m - 1)
                for h in range(HALVES):
                    mm = nc.tensor.matmul(b_w[hg][:, P * b:P * (b + 1)], V[:, b, h, P * hg:P * (hg + 1)],
                                          ET[:, i % 2, h, :], start=(h == 0), stop=(h == HALVES - 1),
                                          skip_group_check=True)
                mm.then_inc(pv_mm, 1)
                return 4 * HALVES * P

            def project(m):
                pe.wait_ge(o_done, VHEADS * (m + 1))
                pe.wait_ge(o_act, (HEADS - VHEADS) * (m + 1))
                for hg in range(HG):
                    mm = nc.tensor.matmul(b_t[0:C, 0:P], AW[:, AW_OUT + C * hg:AW_OUT + C * (hg + 1)],
                                          O[:, hg, :, :], start=(hg == 0), stop=(hg == HG - 1))
                mm.then_inc(yf_mm, 1)
                for hg in range(HG):
                    mm = nc.tensor.matmul(b_pv[:, 0:C], O[:, hg, :, :].rearrange("p b t -> p (b t)"),
                                          AW[:, AW_OUT + C * hg:AW_OUT + C * (hg + 1)], start=(hg == 0), stop=(hg == HG - 1))
                mm.then_inc(y_mm, 1)
                return 4 * HG * 2 * P

            def widen(m):
                pe.wait_ge(ay_done, m + 1)
                for half, dst in enumerate((b_t, b_pv)):
                    if half == 1:
                        pe.wait_ge(r_done, 2 * m + 1)
                    for j in range(FT):
                        w = AW_W1 + P * (FT * half + j)
                        mm = nc.tensor.matmul(dst[:, P * j:P * (j + 1)], AW[:, w:w + P], AY[:], start=True, stop=True)
                    mm.then_inc(h_mm, 1)
                return 4 * 2 * FT * P

            def narrow(m):
                for j in range(FT):
                    pe.wait_ge(ff_done, FT * m + j + 1)
                    if j == 0:
                        pe.wait_ge(ge_done, m + 1)
                    mm = nc.tensor.matmul(b_t[:, 0:C], FF[:, j, :], AW[:, AW_W2 + C * j:AW_W2 + C * (j + 1)],
                                          start=(j == 0), stop=(j == FT - 1))
                mm.then_inc(ff_mm, 1)
                return 4 * FT * P

            def turn_input(m):
                pe.wait_ge(ln3_done, m + 1)
                nc.tensor.transpose(b_t[0:C, 0:P], LN3[:], ident).then_inc(xt_mm, 1)
                return 2 * P

            def turn_states(m):
                pe.wait_ge(hf_done, 2 * (m + 1))
                pe.wait_ge(xt_done, min(m + 2, NT))
                nc.tensor.transpose(b_t[:, 0:C], HF[:].rearrange("p b s -> p (b s)"), ident[0:C, 0:C]).then_inc(out_mm, 1)
                return 2 * P

            def beside(g):
                cols = 0
                for m, o in at(g):
                    if o == QUERIES:
                        cols += queries(m)
                    if m == 0 and o in VALUES_AT:
                        values(VALUES_AT.index(o))
                    ahead = 2 if m == 0 else 0
                    if o + ahead in range(0, 2 * NU, 2):
                        cols += scores(m, (o + ahead) // 2)
                    if o in range(3, 3 + 2 * NU, 2):
                        cols += turn_probs(m, (o - 3) // 2)
                    if o in range(5, 5 + 2 * NU, 2):
                        cols += weigh(m, (o - 5) // 2)
                    if o == PROJECT:
                        cols += project(m)
                    if o == WIDEN:
                        cols += widen(m)
                    if o == NARROW:
                        cols += narrow(m)
                    if o == CELL_INPUT:
                        cols += turn_input(m)
                if leaving(g) is not None:
                    cols += turn_states(leaving(g))
                return cols

            def preload(s, gate, dst, width, off, first):
                m, c = divmod(s // CHUNK, STEPS // CHUNK)
                o = dst[0:C, 0:CHUNK * width].rearrange("p (s q) -> p s q", q=width)[:, :, off:off + B]
                r = XT[:, m, :, CHUNK * c:CHUNK * (c + 1)].rearrange("p b s -> p s b")
                nc.tensor.matmul(o, UW[:, gate, :], r, start=first, stop=True, skip_group_check=True)

            def preload_ig(s):
                if s >= 1:
                    pe.wait_ge(gates, s)
                pe.wait_ge(xt_done, s // STEPS + 1)
                preload(s, 0, b_ig, 2 * B, 0, True)
                preload(s, 1, b_ig, 2 * B, B, False)

            for g in EVERY:
                if g == 0:
                    pe.wait_ge(lw_done, 6)
                    pe.wait_ge(zeroed, 10)
                    preload_ig(0)
                if 0 <= g < LAST:
                    sc = g % CHUNK
                    if g >= 1:
                        pe.wait_ge(h_done, g)
                    for gate in range(2):
                        for r in (slice(0, HC), slice(HC, C)):
                            mm = nc.tensor.matmul(b_ig[r, 8 * sc + 4 * gate:8 * sc + 4 * gate + 4], VW[:, gate, r],
                                                  H[:, g % STEPS, :], start=False, stop=True, skip_group_check=True)
                    mm.then_inc(ig_mm, 1)
                    cols = 0
                    if sc == 0:
                        preload(g, 2, b_o, B, 0, True)
                        cols = 4 * CHUNK * B
                    nc.tensor.matmul(b_o[0:C, 4 * sc:4 * sc + 4], VW[:, 2, :], H[:, g % STEPS, :], start=False,
                                     stop=True, skip_group_check=True).then_inc(o_mm, 1)
                else:
                    cols = 0
                cols += beside(g)
                if any(o in (EXP_TABLE, GELU_TABLE) for _, o in at(g)):
                    cols -= COLS_TABLE
                if 0 <= g < LAST:
                    if (g + 1) % CHUNK == 0 and g + 1 < LAST:
                        fill(COLS_STEP // 3 - cols, b_fill)
                        preload_ig(g + 1)
                    else:
                        fill(COLS_STEP - cols, b_fill)
                elif start(0) + HEADS_1 <= g < 0:
                    fill(COLS_EARLY - cols, b_fill)

        @block.scalar
        def _(act):
            act.dma_start(K[:], consts).then_inc(ld_k, 16)
            act.dma_start(X[:], x_fm).then_inc(ld_x1, 16)
            act.dma_start(LW[:], lstm_w).then_inc(ld_lw, 16)

            act.wait_ge(gn_rs, 1)
            act.wait_ge(xn_done, 2)
            for j in range(2):
                nc.scalar.copy(XC[:, j, :].rearrange("p (y x) -> p y x", y=SIDE), XN[:, j, 1:SIDE + 1, 1:SIDE + 1]
                               ).then_inc(xc_done, 1)

            def z_out(i):
                b, pt = divmod(i, 2)
                for m in range(2):
                    act.wait_ge(z_mm, 2 * i + m + 1)
                    nc.scalar.copy(Z[:, pt, b, :, :].rearrange("p k f -> p (k f)")[:, ZC * m:ZC * (m + 1)],
                                   b_z[2 * (i % 3) + m][:, 0:ZC]).then_inc(z_sb, 1)

            act.wait_ge(om_mm, 1)
            for j in range(2):
                nc.scalar.activation(OM[:, j, :], b_om[0:OFFS2, N * j:N * (j + 1)], ACT.Identity, bias=OB
                                     ).then_inc(om_low, 1)
            z_out(0)
            act.wait_ge(omt_done, 1)
            for i in range(4):
                j, h = divmod(i, 2)
                src = b_omt[:, OFFS2 * i:OFFS2 * (i + 1)].rearrange("p (b o) -> p b o", b=2)[:, :, 18:27]
                nc.scalar.activation(MK[:, 2 * j:2 * j + 2, :, h], src, ACT.Tanh, scale=0.5).then_inc(mask_act, 1)
            def hats_abs(b):
                v = HAT[:, :, b, :, :, :].rearrange("p d k h v -> p d (k h v)")
                act.wait_ge(dist, b + 1)
                nc.scalar.activation(v, v, ACT.Abs).then_inc(hat_abs, 1)

            def hats_relu(b):
                v = HAT[:, :, b, :, :, :].rearrange("p d k h v -> p d (k h v)")
                act.wait_ge(hat_abs, b + 1)
                nc.scalar.activation(v, v, ACT.Relu, bias=1.0, scale=-1.0).then_inc(hat_act, 1)

            z_out(1)
            z_out(2)
            hats_abs(0)
            hats_relu(0)
            for i in range(3, 2 * B):
                z_out(i)
            for g, (b, k) in enumerate(GROUPS):
                if k == HATS_AT and b + 1 < B:
                    hats_abs(b + 1)
                if k == HATS_AT + 2 and b + 1 < B:
                    hats_relu(b + 1)
                act.wait_ge(at_mm, g + 1)
                if g >= 4:
                    act.wait_ge(cv_mm, g - 3)
                nc.scalar.copy(AT[:, g % 4, :, :, :].rearrange("p a h q -> p (a h q)"), b_at[g % 3][:]
                               ).then_inc(at_sb, 1)
            act.wait_ge(zeroed, 10)
            act.wait_ge(t0_mm, 2)
            nc.scalar.copy(T0[:, 4:8, :].rearrange("p n c -> p (n c)"), b_t0[1][:, 0:4 * C]).then_inc(t0_sb, 1)
            act.wait_ge(ln0_st, 1)
            nc.scalar.copy(T0[:, 0:4, :].rearrange("p n c -> p (n c)"), b_t0[0][:, 0:4 * C]).then_inc(t0_sb, 1)
            for i in range(2):
                act.wait_ge(yt_mm, i + 1)
                nc.scalar.copy(YF[0:C, :, P * i:P * (i + 1)].rearrange("p b (n t) -> p n b t", n=4),
                               banks[1 + i][0:C, :].rearrange("p (n b t) -> p n b t", n=4, b=B)).then_inc(yf_done, 1)
            for i in range(4):
                hg, m = divmod(i, 2)
                act.wait_ge(k_mm, i + 1)
                nc.scalar.copy(KF[:, hg, 2 * m:2 * m + 2, :].rearrange("p b q -> p (b q)"), banks[3 + i][:]
                               ).then_inc(k_sb, 1)

            def blocks(m, hg, heads):
                act.wait_ge(q_mm, m + 1)
                if m >= 1:
                    act.wait_ge(s_mm, NU * m)
                for h in heads:
                    r = slice(HD * h, HD * (h + 1))
                    nc.scalar.mul(QB[r, hg, :, h, :], b_et[r, P * hg:P * (hg + 1)].rearrange("p (b t) -> p b t", b=B),
                                  HD ** -0.5).then_inc(q_done, 1)

            def exponents(m, u):
                i = NU * m + u
                act.wait_ge(s_max, i + 1)
                if i >= 2:
                    act.wait_ge(et_mm, i - 1)
                nc.scalar.activation(E[:, i % 2, :], b_s[i % 2][:, 0:N], ACT.Exp, bias=nmax[:, i % 2:i % 2 + 1],
                                     accum_out=rsum[:, i % 2:i % 2 + 1]).then_inc(e_done, 1)

            def turned(m, u):
                i = NU * m + u
                act.wait_ge(et_mm, i + 1)
                if i >= 2:
                    act.wait_ge(pv_mm, i - 1)
                nc.scalar.copy(ET[:, i % 2, :, :].rearrange("p h q -> p (h q)"), b_et[:, 0:N]).then_inc(et_sb, 1)

            def head_out(m, hg, h):
                act.wait_ge(pv_mm, NU * m + B * (hg + 1))
                if m >= 1:
                    act.wait_ge(y_mm, m)
                r = slice(HD * h, HD * (h + 1))
                nc.scalar.copy(O[r, hg, :, :], b_w[hg][r, :].rearrange("p (b h t) -> p b h t", b=B, h=HPG)[:, :, h, :]
                               ).then_inc(o_act, 1)

            def table_for(function):
                nc.scalar.activation(scrap[:], half_neg[0:1, 0:1], function)

            def gelu(m):
                act.wait_ge(h_mm, 2 * m + 1)
                nc.scalar.activation(GE[:].rearrange("p j q -> p (j q)"), b_t[:, 0:FT * P], ACT.Gelu).then_inc(ge_done, 1)

            act.wait_ge(zeroed, 10)
            for g in EVERY:
                if 0 <= g < LAST:
                    sc = g % CHUNK
                    act.wait_ge(ig_mm, g + 1)
                    nc.scalar.activation(SA[:, 0, :, 1:3].rearrange("p b g -> p g b"),
                                         b_ig[0:C, 8 * sc:8 * sc + 8].rearrange("p (g b) -> p g b", g=2),
                                         ACT.Tanh).then_inc(gates, 1)
                    act.wait_ge(o_mm, g + 1)
                    nc.scalar.activation(TO[:], b_o[0:C, 4 * sc:4 * sc + 4], ACT.Tanh).then_inc(o_gate, 1)
                    act.wait_ge(cell, g + 1)
                    nc.scalar.activation(TC, CS[:, :, 2], ACT.Tanh, scale=0.5).then_inc(tanh_c, 1)
                for m, o in at(g):
                    if o in range(BLOCKS, 0):
                        hg, part = divmod(o - BLOCKS, 2)
                        blocks(m, hg, range(2 * part, 2 * part + 2))
                    if o == EXP_TABLE:
                        table_for(ACT.Exp)
                    if o in range(1, 1 + 2 * NU, 2):
                        exponents(m, (o - 1) // 2)
                    if m == 0 and o in VALUES_OUT_AT[2:]:
                        b = VALUES_OUT_AT.index(o)
                        act.wait_ge(v_mm, b + 1)
                        nc.scalar.copy(V[:, b, :, :].rearrange("p h d -> p (h d)"), b_v[b][:]).then_inc(v_sb, 1)
                    if o in range(4, 4 + 2 * NU, 2):
                        turned(m, (o - 4) // 2)
                    if o == HEADS_1:
                        head_out(m, 1, 2)
                        head_out(m, 1, 3)
                    if o == GELU_TABLE:
                        table_for(ACT.Gelu)
                    if o == GELU:
                        gelu(m)

        @block.vector
        def _(dve):
            def link(ins, n=[0]):
                n[0] += 1
                ins.then_inc(v_link, 1)
                dve.wait_ge(v_link, n[0])

            nc.vector.memset(FB[:], 0.0).then_inc(fb_zero, 1)
            dve.wait_ge(ld_x, 16)
            for j in range(2):
                ins = nc.vector.bn_stats(gstat[:, j, :], X2[:, j, :])
            link(ins)
            for j in range(2):
                ins = nc.vector.bn_aggr(gmv[:, j, :], gstat[:, j, :])
            link(ins)
            nc.vector.tensor_copy(gme[:, :, 0:1], gmv[:, :, 0:1]).then_inc(gn_sent, 1)
            link(nc.vector.tensor_tensor(gsq[:], gmv[:, :, 0:1], gmv[:, :, 0:1], ALU.mult))
            nc.vector.tensor_tensor(gme[:, :, 1:2], gsq[:], gmv[:, :, 1:2], ALU.add).then_inc(gn_sent, 1)
            dve.wait_ge(gn_avg, 1)
            link(nc.vector.tensor_copy(gmv[:].rearrange("p j s -> p (j s)"), b_misc[:, 0:4]))
            link(nc.vector.tensor_tensor(gsq[:], gmv[:, :, 0:1], gmv[:, :, 0:1], ALU.mult))
            nc.vector.tensor_tensor(gvar[:], gmv[:, :, 1:2], gsq[:], ALU.subtract).then_inc(gn_var, 1)
            dve.wait_ge(zeroed, 10)
            dve.wait_ge(gn_rs, 1)
            for j in range(2):
                nc.vector.tensor_scalar(XN[:, j, 1:SIDE + 1, 1:SIDE + 1],
                                        X2[:, j, :].rearrange("p (y x) -> p y x", y=SIDE),
                                        gmv[:, j, 0:1], grs[:, j, :], ALU.subtract, ALU.mult).then_inc(xn_done, 1)
            for j in range(2):
                dve.wait_ge(om_low, j + 1)
                nc.vector.tensor_tensor(OM[:, j, :], b_om[C:C + OFFS2, N * j:N * (j + 1)], OM[:, j, :], ALU.add
                                        ).then_inc(om_sb, 1)
            dve.wait_ge(ld_k, 16)
            dve.wait_ge(omt_done, 1)
            dve.wait_ge(mask_act, 4)
            for i in range(4):
                j, h = divmod(i, 2)
                src = b_omt[:, OFFS2 * i:OFFS2 * (i + 1)].rearrange("p (b o) -> p b o", b=2)[:, :, 0:18].rearrange(
                    "p b (k d) -> p b k d", d=2)
                for bb in range(2):
                    ins = nc.vector.tensor_tensor(POS[:, :, 2 * j + bb, :, h].rearrange("p d k -> p k d"),
                                                  src[:, bb], base[:, h], ALU.add)
            link(ins)
            pos = POS[:].rearrange("p d b k h -> p (d b k h)")
            nc.vector.tensor_scalar(MK[:], MK[:], 0.5, 0.5, ALU.mult, ALU.add)
            link(nc.vector.tensor_scalar(pos, pos, 0.0, float(SIDE + 1), ALU.max, ALU.min))
            def distances(b):
                kh = TAPS * HALVES
                p_b = POS[:, :, b, :, :].rearrange("p d k h -> p d (k h)")
                nc.vector.tensor_tensor(HAT[:, :, b, :, :, :].rearrange("p d k h v -> p d (k h) v"),
                                        p_b[:, :, :, None].to_broadcast([P, 2, kh, SIDE]),
                                        grid[:, None, None, :].to_broadcast([P, 2, kh, SIDE]),
                                        ALU.subtract).then_inc(dist, 1)

            def masked(b):
                dve.wait_ge(hat_act, b + 1)
                v = HAT[:, 0, b, :, :, :].rearrange("p k h v -> p (k h) v")
                m = MK[:, b, :, :].rearrange("p k h -> p (k h)")
                link(nc.vector.tensor_tensor(v, v, m[:, :, None].to_broadcast([P, TAPS * HALVES, SIDE]), ALU.mult))

            def sampled(b):
                dve.wait_ge(cv_mm, TAPS * (b + 1))
                if b == 0:
                    dve.wait_ge(ld_x1, 16)
                low, high = (b_cv[b % 2][C * i:C * (i + 1), 0:N].rearrange("p (n t) -> p n t", t=TT) for i in range(2))
                nc.vector.tensor_tensor(T0F[:, :, b, :], low, X[:, b, :].rearrange("p (n t) -> p n t", t=TT), ALU.add
                                        ).then_inc(t0f_done, 1)
                dve.wait_ge(t0f_done, 2 * b + 1)
                nc.vector.tensor_tensor(T0F[:, :, b, :], high, T0F[:, :, b, :], ALU.add).then_inc(t0f_done, 1)

            distances(0)
            distances(1)
            for g, (b, k) in enumerate(GROUPS):
                if k == 0:
                    masked(b)
                if k == 3 and b + 2 < B:
                    distances(b + 2)
                if g >= 4:
                    dve.wait_ge(at_mm, g - 3)
                sh = [P, HALVES, SIDE, SIDE]
                nc.vector.tensor_tensor(A[:, g % 4, :, :].rearrange("p h (y x) -> p h y x", y=SIDE),
                                        HAT[:, 0, b, k, :, :, None].to_broadcast(sh),
                                        HAT[:, 1, b, k, :, None, :].to_broadcast(sh), ALU.mult).then_inc(a_done, 1)
                if k == 7 and b >= 1:
                    sampled(b - 1)
            sampled(B - 1)

            for i in range(2):
                if i == 0:
                    dve.wait_ge(t0_mm, 1)
                else:
                    dve.wait_ge(t0_sb, 1)
                for n in range(4 * i, 4 * i + 4):
                    tokens = b_t0[0][:, C * n:C * (n + 1)] if i == 0 else T0[:, n, :]
                    ins = nc.vector.bn_stats(st0[:, n, :], tokens)
                ins.then_inc(ln0_st, 1)
                dve.wait_ge(ln0_st, i + 1)
                for n in range(4 * i, 4 * i + 4):
                    nc.vector.bn_aggr(mv0[:, n, :], st0[:, n, :]).then_inc(ln0_mv, 1)
            dve.wait_ge(t0_sb, 2)
            for n in range(NT):
                if n % 4 == 0:
                    dve.wait_ge(ln0_rs, n // 4 + 1)
                nc.vector.tensor_scalar(Y[:, n, :], T0[:, n, :], mv0[:, n, 0:1], rs0[:, n, :], ALU.subtract,
                                        ALU.mult).then_inc(y_done, 1)
            dve.wait_ge(yb_done, 2)

            def values_out(b):
                dve.wait_ge(v_mm, b + 1)
                nc.vector.tensor_copy(V[:, b, :, :].rearrange("p h d -> p (h d)"), b_v[b][:]).then_inc(v_sb, 1)

            def largest(m, u):
                i = NU * m + u
                dve.wait_ge(s_mm, i + 1)
                nc.vector.tensor_reduce(nmax[:, i % 2:i % 2 + 1], b_s[i % 2][:, 0:N], AX.X, ALU.max, negate=True
                                        ).then_inc(s_max, 1)

            def inverse_sum(m, u):
                i = NU * m + u
                dve.wait_ge(e_done, i + 1)
                nc.vector.reciprocal(rinv[:, i % 2:i % 2 + 1], rsum[:, i % 2:i % 2 + 1]).then_inc(e_inv, 1)

            def normalised(m, u):
                i = NU * m + u
                dve.wait_ge(e_inv, i + 1)
                nc.vector.tensor_scalar(E[:, i % 2, :], E[:, i % 2, :], rinv[:, i % 2:i % 2 + 1], None, ALU.mult
                                        ).then_inc(e_norm, 1)

            def head_out(m, hg, h):
                dve.wait_ge(pv_mm, NU * m + B * (hg + 1))
                r = slice(HD * h, HD * (h + 1))
                nc.vector.tensor_copy(O[r, hg, :, :], b_w[hg][r, :].rearrange("p (b h t) -> p b h t", b=B, h=HPG)[:, :, h, :]
                                      ).then_inc(o_done, 1)

            def gated(m, j):
                dve.wait_ge(ge_done, m + 1)
                dve.wait_ge(h_mm, 2 * m + 2)
                nc.vector.tensor_tensor(FF[:, j, :], b_pv[:, P * j:P * (j + 1)], GE[:, j, :], ALU.mult
                                        ).then_inc(ff_done, 1)

            def norm_stats(m, j, src):
                nc.vector.bn_stats(st[:, j, :], src).then_inc(st_done, 1)

            def norm_aggr(m, j):
                dve.wait_ge(st_done, 3 * m + j + 1)
                nc.vector.bn_aggr(mv[:, j, :], st[:, j, :]).then_inc(t_mv, 1)

            def norm_apply(m, j, dst, src):
                dve.wait_ge(t_rs, 3 * m + j + 1)
                return nc.vector.tensor_scalar(dst, src, mv[:, j, 0:1], rs[:, j, :], ALU.subtract, ALU.mult)

            def first(g):
                for m, o in at(g):
                    if m == 0 and o in VALUES_OUT_AT[:2]:
                        values_out(VALUES_OUT_AT.index(o))
                    if m == 0 and o == VALUES_OUT_AT[-1] + 3:
                        dve.wait_ge(v_sb, B)
                        nc.vector.memset(CS, 0.0).then_inc(cs_zero, 1)
                    if m == 0 and o in range(0, 2 * NU, 2):
                        largest(m, o // 2)
                    if m > 0 and o in range(1, 1 + 2 * NU, 2):
                        largest(m, (o - 1) // 2)
                    if o in range(2, 2 + 2 * NU, 2):
                        inverse_sum(m, (o - 2) // 2)
                    if o == AGGR[0]:
                        dve.wait_ge(r_done, 2 * m + 1)
                        norm_stats(m, 0, R1[:])
                    if o == NORM_1:
                        norm_apply(m, 0, X1[:], R1[:]).then_inc(t_link, 1)
                    if o == NARROWED:
                        dve.wait_ge(ff_mm, m + 1)
                        dve.wait_ge(t_link, 5 * m + 3)
                        nc.vector.tensor_tensor(R2[:], b_t[:, 0:C], X1[:], ALU.add).then_inc(r_done, 1)
                    if o == NORM_2:
                        norm_apply(m, 1, R2[:], R2[:]).then_inc(t_link, 1)
                    if o == TOKENS:
                        dve.wait_ge(t_link, 5 * m + 5)
                        nc.vector.tensor_tensor(T1[:, m, :], R2[:], TB[:, m, :], ALU.add).then_inc(t1_done, 1)
                    if o == CELL_INPUT:
                        norm_apply(m, 2, LN3[:], T1[:, m, :]).then_inc(ln3_done, 1)
                    if o == CELL_READY:
                        dve.wait_ge(xt_mm, m + 1)
                        nc.vector.tensor_copy(XT[0:C, m, :, :].rearrange("p b t -> p (b t)"), b_t[0:C, 0:P]
                                              ).then_inc(xt_done, 1)
                if g == LAST:
                    dve.wait_ge(h_done, LAST)
                    dve.wait_ge(out_mm, NT - 1)
                    nc.vector.tensor_copy(HF[:, :, 0:STEPS - 1], H[0:C, 1:STEPS, :].rearrange("p s b -> p b s")
                                          ).then_inc(hf_done, 1)
                    nc.vector.tensor_copy(HF[:, :, STEPS - 1], H[0:C, 0, :]).then_inc(hf_done, 1)
                if leaving(g - 1) is not None:
                    m = leaving(g - 1)
                    dve.wait_ge(out_mm, m + 1)
                    if m >= 2:
                        dve.wait_ge(stored, 16 * (m - 1))
                    nc.vector.scalar_tensor_tensor(out=OUT[:, m % 2, :], in0=b_t[:, 0:C], scalar=0.5, in1=T1[:, m, :],
                                                   op0=ALU.mult, op1=ALU.add).then_inc(out_add, 1)

            def second(g):
                for m, o in at(g):
                    if o == HEADS_1:
                        head_out(m, 1, 0)
                    if o == PROJECTED:
                        dve.wait_ge(yf_mm, m + 1)
                        nc.vector.tensor_scalar(AY[0:C, :], b_t[0:C, 0:P], AW[0:C, AW_BO:AW_BO + 1], None, ALU.add
                                                ).then_inc(ay_done, 1)
                    if o == AGGR[0]:
                        norm_aggr(m, 0)
                    if o == GATED:
                        gated(m, 0)
                    if o == AGGR[1]:
                        norm_aggr(m, 1)
                    if o == AGGR[2]:
                        norm_aggr(m, 2)

            def third(g):
                for m, o in at(g):
                    if o == GATED:
                        gated(m, 1)
                    if o in range(2, 2 + 2 * NU, 2):
                        normalised(m, (o - 2) // 2)
                    if o in range(HEADS_0, HEADS_0 + 2 * HPG, 2):
                        head_out(m, 0, (o - HEADS_0) // 2)
                    if o == HEADS_1:
                        head_out(m, 1, 1)
                    if o == PROJECTED:
                        dve.wait_ge(y_mm, m + 1)
                        nc.vector.tensor_tensor(R1[:], b_pv[:, 0:C], YB[:, m, :], ALU.add).then_inc(r_done, 1)
                    if o == NORM_1:
                        dve.wait_ge(t_link, 5 * m + 1)
                        nc.vector.tensor_tensor(X1[:], X1[:], VEC[:, VEC_G1, :], ALU.mult).then_inc(t_link, 1)
                    if o == GATED:
                        dve.wait_ge(t_link, 5 * m + 2)
                        nc.vector.tensor_tensor(X1[:], X1[:], VEC[:, VEC_B1, :], ALU.add).then_inc(t_link, 1)
                    if o == NARROWED:
                        dve.wait_ge(r_done, 2 * m + 2)
                        norm_stats(m, 1, R2[:])
                    if o == NORM_2:
                        dve.wait_ge(t_link, 5 * m + 4)
                        nc.vector.tensor_tensor(R2[:], R2[:], VEC[:, VEC_G2, :], ALU.mult).then_inc(t_link, 1)
                    if o == TOKENS:
                        dve.wait_ge(t1_done, m + 1)
                        norm_stats(m, 2, T1[:, m, :])

            for g in EVERY:
                cell_step = 0 <= g < LAST
                first(g)
                if cell_step:
                    if g >= 1:
                        dve.wait_ge(h_done, g)
                    else:
                        dve.wait_ge(cs_zero, 1)
                    nc.vector.scalar_tensor_tensor(out=SA[:, 1, :, 2], in0=H[0:C, g % STEPS, :], scalar=0.5,
                                                   in1=CS[:, :, 2], op0=ALU.mult, op1=ALU.mult).then_inc(u_done, 1)
                second(g)
                if cell_step:
                    dve.wait_ge(gates, g + 1)
                    dve.wait_ge(u_done, g + 1)
                    nc.vector.tensor_tensor_scan(CS.rearrange("p b q -> p (b q)"),
                                                 SA[:, 0, :, :].rearrange("p b q -> p (b q)"),
                                                 SA[:, 1, :, :].rearrange("p b q -> p (b q)"), 0.0,
                                                 op0=ALU.mult, op1=ALU.add).then_inc(cell, 1)
                third(g)
                if cell_step:
                    dve.wait_ge(tanh_c, g + 1)
                    dve.wait_ge(o_gate, g + 1)
                    if g % STEPS == 0 and g >= STEPS:
                        dve.wait_ge(hf_done, 2 * (g // STEPS))
                    nc.vector.scalar_tensor_tensor(out=H[0:C, (g + 1) % STEPS, :], in0=TO[:], scalar=1.0, in1=TC,
                                                   op0=ALU.add, op1=ALU.mult).then_inc(h_done, 1)


def shape_constants():
    k = np.zeros((P, K_END), np.float32)
    p = np.arange(P)
    k[p, K_ID + p] = 1.0
    k[:, K_PAIR:K_PAIR + P] = np.where(p[:, None] // 2 == p[None, :] // 2, 0.5, 0.0)
    base = np.zeros((P, HALVES, TAPS, 2), np.float32)
    for h in range(HALVES):
        for t in range(TAPS):
            base[:, h, t, 0] = (P * h + p) // SIDE + 1 + t // 3 - 1
            base[:, h, t, 1] = p % SIDE + 1 + t % 3 - 1
    k[:, K_BASE:K_GRID] = base.reshape(P, 36)
    k[:, K_GRID:K_GRID + SIDE] = np.arange(1, SIDE + 1)
    return k


def packed(i):
    f = {n: np.asarray(a) for n, a in i.items()}
    x = f["x"].reshape(B // 2, 2, N, C)
    a = {}
    a["x_fm2"] = np.ascontiguousarray(x.transpose(1, 3, 0, 2).reshape(P, 2, N))
    a["x_fm"] = np.ascontiguousarray(f["x"].reshape(B, N, C).transpose(2, 0, 1))
    cw = np.zeros((P, CW_END), np.float32)
    ow = f["L0_conv_offset_w"].reshape(TAPS, C, OFFS).transpose(1, 0, 2)
    dcn = np.zeros((P, 2, TAPS * C), np.float32)
    dw = f["L0_conv_dcn_weight"].transpose(1, 2, 3, 0).reshape(C, TAPS * C)
    for h in range(2):
        r = slice(C * h, C * (h + 1))
        cw[r, 0:CW_OB].reshape(C, TAPS, 2, OFFS)[:, :, h, :] = ow
        dcn[r, h] = dw
        cw[OFFS * h:OFFS * (h + 1), CW_OB] = f["L0_conv_offset_b"].reshape(OFFS)
    a["conv_w"] = cw
    a["dcn_w"] = dcn
    aw = np.zeros((P, AW_END), np.float32)
    aw[0:C, AW_QKV:AW_OUT] = f["L1_attn_w_qkv"].T
    aw[:, AW_OUT:AW_W1] = f["L1_attn_w_out"].T.reshape(HG, P, C).transpose(1, 0, 2).reshape(P, HG * C)
    aw[0:C, AW_W1:AW_WV] = f["L1_attn_w1"].T
    aw[0:C, AW_WV:AW_W2] = f["L1_attn_wv"].T
    aw[:, AW_W2:AW_BO] = f["L1_attn_w2"].T.reshape(FT, P, C).transpose(1, 0, 2).reshape(P, FT * C)
    aw[0:C, AW_BO] = f["L1_attn_b_out"]
    a["attn_w"] = aw
    lw = np.zeros((C + 1, LW_END), np.float32)
    for j, g in enumerate("ico"):
        lw[0:C, LW_V + C * j:LW_V + C * (j + 1)] = f[f"L1_ffn_V_{g}"]
        lw[0:C, LW_U + C * j:LW_U + C * (j + 1)] = f[f"L1_ffn_U_{g}"]
        lw[C, LW_U + C * j:LW_U + C * (j + 1)] = f[f"L1_ffn_b_{g}"]
    a["lstm_w"] = lw
    a["vecs"] = np.stack([f[f"L1_attn_{n}"] for n in ("b_out", "ln1_g", "ln1_b", "ln2_g", "ln2_b")])
    a["consts"] = shape_constants()
    return a


def kernel(**inputs):
    import concourse.bacc as _bacc
    from concourse.bass_utils import run_bass_kernel_spmd as _run

    nc = _bacc.Bacc("TRN2", target_bir_lowering=False, num_devices=1)
    arrays = packed(inputs)
    args = [nc.dram_tensor(f"in_{n}", a.shape, F32, kind="ExternalInput").ap() for n, a in arrays.items()]
    out = nc.dram_tensor("out_0_dram", (NT, P, C), F32, kind="ExternalOutput").ap()
    hybrid_kernel(nc, *args, out)
    r = _run(nc, [{f"in_{n}": a for n, a in arrays.items()}], core_ids=[0])
    tiles = r.results[0]["out_0_dram"].reshape(NT, B, TT, C)
    return tiles.transpose(1, 0, 2, 3).reshape(B, SIDE, SIDE, C)
```
